# Optimizing a Trainium2 kernel written in Bass

```python
import numpy as np
import jax
import jax.numpy as jnp

def _softmax(x, axis=-1):
    return jax.nn.softmax(x, axis=axis)

def _gelu(x):
    return jax.nn.gelu(x, approximate=True)

def _silu(x):
    return jax.nn.silu(x)

def _sigmoid(x):
    return jax.nn.sigmoid(x)

def _layernorm(x, axis=-1, eps=1e-05):
    m = jnp.mean(x, axis=axis, keepdims=True)
    v = jnp.var(x, axis=axis, keepdims=True)
    return (x - m) / jnp.sqrt(v + eps)

def _scatter_add(tgt, idx, src, axis=0):
    return tgt.at[idx].add(src)

def _segment_sum(src, seg, n):
    return jax.ops.segment_sum(src, seg, n)
kernel_name = 'mk_seq_postln_d1_jaxref_r8_4d3ddc'

def setup_inputs(seed: int=0):
    np.random.seed(seed)
    _w = jnp.asarray

    def _L0_attn_setup():
        import jax, jax.numpy as jnp
        import numpy as np
        B, S, D_IN, D_OUT, H = (2, 256, 128, 128, 16)
        HD = D_OUT // H
        key = jax.random.key(seed)
        ks = jax.random.split(key, 6)
        x = jax.random.normal(ks[0], (B, S, D_IN), jnp.float32)
        Wq = jax.random.normal(ks[1], (D_IN, D_OUT), jnp.float32) * 0.02
        Wk = jax.random.normal(ks[2], (D_IN, D_OUT), jnp.float32) * 0.02
        Wv = jax.random.normal(ks[3], (D_IN, D_OUT), jnp.float32) * 0.02
        Wo = jax.random.normal(ks[4], (D_OUT, D_OUT), jnp.float32) * 0.02
        bo = jax.random.normal(ks[5], (D_OUT,), jnp.float32) * 0.02
        return {'x': x, 'Wq': Wq, 'Wk': Wk, 'Wv': Wv, 'Wo': Wo, 'bo': bo}
    _L0_attn_in = _L0_attn_setup()

    def _L0_ffn_setup():
        import jax, jax.numpy as jnp
        import numpy as np
        B, N, D, E, MULT = (4, 256, 128, 8, 4)
        F = D * MULT

        def _top2_gate(xn, Wg):
            logits = jnp.einsum('bnd,ed->bne', xn, Wg)
            probs = jax.nn.softmax(logits, axis=-1)
            top1 = jnp.argmax(probs, axis=-1)
            t1v = jnp.take_along_axis(probs, top1[..., None], axis=-1)[..., 0]
            masked = jnp.where(jax.nn.one_hot(top1, probs.shape[-1], dtype=bool), -jnp.inf, probs)
            top2 = jnp.argmax(masked, axis=-1)
            t2v = jnp.take_along_axis(masked, top2[..., None], axis=-1)[..., 0]
            denom = t1v + t2v + 1e-09
            combine = jnp.stack([t1v / denom, t2v / denom], axis=-1)
            idx = jnp.stack([top1, top2], axis=-1)
            return (combine, idx)
        key = jax.random.key(seed)
        ks = jax.random.split(key, 8)
        s_in = 1.0 / np.sqrt(D)
        s_hid = 1.0 / np.sqrt(F)
        return {'x': jax.random.normal(ks[0], (B, N, D), dtype=jnp.float32), 'gamma': jnp.ones((D,), dtype=jnp.float32), 'beta': jnp.zeros((D,), dtype=jnp.float32), 'Wg': jax.random.normal(ks[1], (E, D), dtype=jnp.float32) * s_in, 'W1': jax.random.normal(ks[2], (E, D, F), dtype=jnp.float32) * s_in, 'b1': jax.random.normal(ks[3], (E, F), dtype=jnp.float32) * 0.01, 'W2': jax.random.normal(ks[4], (E, F, D), dtype=jnp.float32) * s_hid, 'b2': jax.random.normal(ks[5], (E, D), dtype=jnp.float32) * 0.01}
    _L0_ffn_in = _L0_ffn_setup()
    _d = {'L0_attn_x': _L0_attn_in['x'], 'L0_attn_Wq': _L0_attn_in['Wq'], 'L0_attn_Wk': _L0_attn_in['Wk'], 'L0_attn_Wv': _L0_attn_in['Wv'], 'L0_attn_Wo': _L0_attn_in['Wo'], 'L0_attn_bo': _L0_attn_in['bo'], 'L0_ffn_gamma': _L0_ffn_in['gamma'], 'L0_ffn_beta': _L0_ffn_in['beta'], 'L0_ffn_Wg': _L0_ffn_in['Wg'], 'L0_ffn_W1': _L0_ffn_in['W1'], 'L0_ffn_b1': _L0_ffn_in['b1'], 'L0_ffn_W2': _L0_ffn_in['W2'], 'L0_ffn_b2': _L0_ffn_in['b2']}
    _x0 = _d['L0_attn_x']
    _d['L0_attn_x'] = jax.random.normal(jax.random.fold_in(jax.random.key(seed), 1), (16, 512, 128), dtype=_x0.dtype)
    del _x0
    return _d

def reference(L0_attn_x, L0_attn_Wq, L0_attn_Wk, L0_attn_Wv, L0_attn_Wo, L0_attn_bo, L0_ffn_gamma, L0_ffn_beta, L0_ffn_Wg, L0_ffn_W1, L0_ffn_b1, L0_ffn_W2, L0_ffn_b2):

    def _L0_attn_ref(x, Wq, Wk, Wv, Wo, bo):
        import jax, jax.numpy as jnp
        import numpy as np
        B, S, D_IN, D_OUT, H = (2, 256, 128, 128, 16)
        HD = D_OUT // H
        b, s, _ = x.shape

        def to_heads(t):
            return t.reshape(b, s, H, HD).transpose(0, 2, 1, 3)
        Q = to_heads(x @ Wq)
        K = to_heads(x @ Wk)
        V = to_heads(x @ Wv)
        scale = 1.0 / jnp.sqrt(jnp.asarray(HD, x.dtype))
        scores = jnp.einsum('bhqd,bhkd->bhqk', Q, K) * scale
        causal_mask = jnp.triu(jnp.ones((s, s), dtype=bool), k=1)
        scores = jnp.where(causal_mask, jnp.asarray(-1000000.0, scores.dtype), scores)
        weights = jax.nn.softmax(scores, axis=-1)
        attn = jnp.einsum('bhqk,bhkd->bhqd', weights, V)
        attn = attn.reshape(b, s, D_OUT)
        return attn @ Wo + bo

    def _L0_ffn_ref(x, gamma, beta, Wg, W1, b1, W2, b2):
        import jax, jax.numpy as jnp
        import numpy as np
        B, N, D, E, MULT = (4, 256, 128, 8, 4)
        F = D * MULT

        def _top2_gate(xn, Wg):
            logits = jnp.einsum('bnd,ed->bne', xn, Wg)
            probs = jax.nn.softmax(logits, axis=-1)
            top1 = jnp.argmax(probs, axis=-1)
            t1v = jnp.take_along_axis(probs, top1[..., None], axis=-1)[..., 0]
            masked = jnp.where(jax.nn.one_hot(top1, probs.shape[-1], dtype=bool), -jnp.inf, probs)
            top2 = jnp.argmax(masked, axis=-1)
            t2v = jnp.take_along_axis(masked, top2[..., None], axis=-1)[..., 0]
            denom = t1v + t2v + 1e-09
            combine = jnp.stack([t1v / denom, t2v / denom], axis=-1)
            idx = jnp.stack([top1, top2], axis=-1)
            return (combine, idx)
        residual = x
        mu = jnp.mean(x, axis=-1, keepdims=True)
        var = jnp.mean(jnp.square(x - mu), axis=-1, keepdims=True)
        xn = (x - mu) / jnp.sqrt(var + 1e-05) * gamma + beta
        combine, idx = _top2_gate(xn, Wg)
        n_expert = Wg.shape[0]
        onehot = jax.nn.one_hot(idx, n_expert, dtype=x.dtype)
        gates = jnp.einsum('bns,bnse->ebn', combine, onehot)

        def body(acc, params):
            w1, b1e, w2, b2e, g = params
            h = jax.nn.gelu(jnp.einsum('bnd,df->bnf', xn, w1) + b1e, approximate=True)
            y = jnp.einsum('bnf,fd->bnd', h, w2) + b2e
            return (acc + g[..., None] * y, None)
        out, _ = jax.lax.scan(body, jnp.zeros_like(x), (W1, b1, W2, b2, gates))
        return residual + out
    x = L0_attn_x
    x = _layernorm(x + _L0_attn_ref(x, L0_attn_Wq, L0_attn_Wk, L0_attn_Wv, L0_attn_Wo, L0_attn_bo), axis=-1)
    x = _layernorm(x + _L0_ffn_ref(x, L0_ffn_gamma, L0_ffn_beta, L0_ffn_Wg, L0_ffn_W1, L0_ffn_b1, L0_ffn_W2, L0_ffn_b2), axis=-1)
    return x

_drawn_inputs = setup_inputs


def setup_inputs(seed=0):
    import zlib

    import numpy as np

    out = dict(_drawn_inputs(seed))
    spreads = {'L0_ffn_gamma': (1.0, 0.2), 'L0_ffn_beta': (0.0, 0.1)}
    factors = {'L0_attn_Wq': 8.0,
     'L0_attn_Wk': 8.0,
     'L0_attn_Wv': 4.989,
     'L0_attn_Wo': 4.59,
     'L0_ffn_b1': 22.705,
     'L0_ffn_b2': 8.0}
    for name, (base, spread) in spreads.items():
        noise = np.random.default_rng([zlib.crc32(name.encode()), seed]).standard_normal(out[name].shape)
        drawn = base * np.exp(spread * noise) if base else spread * noise
        out[name] = jnp.asarray(drawn.astype(out[name].dtype))
    for name, factor in factors.items():
        out[name] = (out[name] * factor).astype(out[name].dtype)
    return out
```

```python
from contextlib import ExitStack

import concourse.bass as bass
from concourse import mybir

F32 = mybir.dt.float32
F32R = mybir.dt.float32r
BF16 = mybir.dt.bfloat16
I32 = mybir.dt.int32
ALU = mybir.AluOpType
ACT = mybir.ActivationFunctionType
AX = mybir.AxisListType

P = 128
HD = 8
EPS = 1e-5
NEG = -1.0e30
SKIP = 1 << 24
ROW = 132


class At:

    def __init__(self, value, parity, loop):
        self.value, self.parity, self.loop = value, parity % 2, loop

    def plus(self, k):
        return At(self.value + k, self.parity + k, self.loop)

    def exists(self, n):
        return self.loop or 0 <= self.value < n


def wait_apart(eng, passed, sem, value):
    eng.wait_ge(sem, value)
    if not isinstance(value, int):
        eng.sem_inc(passed, 1)


def need(eng, sem, per, b, n, passed=None):
    if b.loop or b.value * per + n > 0:
        if passed is None:
            eng.wait_ge(sem, b.value * per + n)
        else:
            wait_apart(eng, passed, sem, b.value * per + n)


def build_program(nc, x, wq, wk, wv, wo, bo, gamma, beta, wg, w1, b1, w2, b2, out):
    NB, S, D = x.shape
    E, _, F = w1.shape
    NH = D // HD
    QB = S // P
    FC = F // P
    T = NB * S
    TOPK = 2
    REG = T + P
    NT = T * TOPK // P + E
    SCALE = float(HD) ** -0.5
    GH = 4
    UNITS = 3 * NH
    AUNITS = 3 * NH // 2
    ROUTE = 20
    WEIGHTS = 3 * 4 + 6
    assert (S, D, NH, QB, FC, E) == (512, 128, 16, 4, 4, 8) and NB % 2 == 0 and NT % 4 == 0

    x_rows = x.rearrange("b s d -> (b s) d")
    out_rows = out.rearrange("b s d -> (b s) d")
    rows_d = nc.dram_tensor("rows_d", (E * REG + E * P, ROW), F32, kind="Internal").ap()
    y_d = nc.dram_tensor("y_d", (T * TOPK, D), F32, kind="Internal").ap()
    qk_d = nc.dram_tensor("qk_d", (2, 2, P, 2, S), F32, kind="Internal").ap()
    att_d = nc.dram_tensor("att_d", (D, S), F32, kind="Internal").ap()
    x2_d = nc.dram_tensor("x2_d", (T, D), F32, kind="Internal").ap()

    with ExitStack() as ctx:
        def sb(name, shape, dt=F32):
            return ctx.enter_context(nc.sbuf_tensor(name, shape, dt))

        def pb(name, shape):
            return ctx.enter_context(nc.psum_tensor(name, shape, F32))

        sems = {}

        def sem(name):
            if name not in sems:
                sems[name] = ctx.enter_context(nc.semaphore(name))
            return sems[name]

        kside = sb("kside", [P, 2, NH, S], F32R)
        qside = sb("qside", [P, 2, NH // GH, S], F32R)
        probs = sb("probs", [P, 8, 1280])
        vpad = sb("vpad", [P, 2, QB, NH, 32])
        xin = sb("xin", [P, 2, QB, D])
        xbo = sb("xbo", [P, 2, QB, D])
        xt = sb("xt", [P, S])
        qhl = sb("qhl", [P, 2, S], F32R)
        khl = sb("khl", [P, 2, S], F32R)
        ucp = sb("ucp", [P, S])
        urec = sb("urec", [P, QB, 8])
        att = sb("att", [P, QB, D])
        attt = sb("attt", [P, S])
        rows16 = sb("rows16", [P, S])
        ysum = sb("ysum", [P, QB, D])
        x1 = sb("x1", [P, QB, D])
        x2 = sb("x2", [P, QB, D])
        xc = sb("xc", [P, QB, D])
        xn = sb("xn", [P, 2, QB, TOPK, ROW])
        xnt = sb("xnt", [P, S])
        negmax = sb("negmax", [P, 2, QB, GH])
        mhl = sb("mhl", [P, QB, 2, GH], F32R)
        mt = sb("mt", [2 * GH, S])
        wq_s, wk_s, wv_s, wo_s = (sb(n, [P, D]) for n in ("wq_s", "wk_s", "wv_s", "wo_s"))
        wgt = sb("wgt", [P, E])
        bo_b, gam_b, bet_b = (sb(n, [P, D]) for n in ("bo_b", "gam_b", "bet_b"))
        ident = sb("ident", [P, P])
        identb = sb("identb", [P, P], BF16)
        maskb = sb("maskb", [P, P], BF16)
        lowerb = sb("lowerb", [P, P], BF16)
        onesb = sb("onesb", [P, P], BF16)
        stats = sb("stats", [P, 2, QB, 6])
        mv = sb("mv", [P, 2, QB, 2])
        rs = sb("rs", [P, 2, 4, QB])
        halfneg = sb("halfneg", [P, QB])
        lg = sb("lg", [P, QB, E])
        rt = sb("rt", [P, 12, QB, E])
        rv = sb("rv", [P, 8, QB])
        onehot = sb("onehot", [P, QB + 1, E], BF16)
        wtab = sb("wtab", [P, QB, E])
        wtab_i = sb("wtab_i", [P, QB, E], I32)
        used = sb("used", [P, E])
        first_row = sb("first_row", [P, E])
        tile_i = sb("tile_i", [P, NT], I32)
        tile_f = sb("tile_f", [P, NT])
        used_i = sb("used_i", [P, E], I32)
        slot = sb("slot", [P, 2, TOPK, QB], I32)
        gates = sb("gates", [P, NB * QB, TOPK])
        dest_i = sb("dest_i", [P, QB, TOPK], I32)
        dest = sb("dest", [P, QB, TOPK])
        w1_s = probs[:, :, :].rearrange("p r n -> p (r n)")[:, 0:E * F].rearrange("p (e f) -> p e f", e=E)
        w2_s = probs[:, :, :].rearrange("p r n -> p (r n)")[:, E * F:2 * E * F].rearrange(
            "p (e c d) -> p e c d", e=E, c=FC)
        w1_t = sb("w1_t", [P, 2, F])
        b1_s = sb("b1_s", [P, E, FC])
        b1_r = sb("b1_r", [E * FC, P])
        b2_b = vpad[:, 1].rearrange("p b h c -> p (b h c)")[:, 0:E * D].rearrange("p (e d) -> p e d", e=E)
        xs = sb("xs", [P, 4, ROW])
        xst = sb("xst", [P, 2, P])
        ht = xbo
        ys = sb("ys", [P, 4, D])
        zrow = sb("zrow", [P, ROW])
        plan = sb("plan", [1, 3, NT])
        plan_i = sb("plan_i", [1, 2, NT], I32)
        cnt = sb("cnt", [1, 8, E])
        cnt_i = sb("cnt_i", [1, 2, E], I32)
        padix = sb("padix", [P, E], I32)
        padf = sb("padf", [P, E])
        iotap = sb("iotap", [P, 1], I32)
        iotapf = sb("iotapf", [P, 1])
        y_t = vpad[:, :, :, :, :].rearrange("p a b h c -> p (a b h c)").rearrange("p (r n) -> p r n", r=4)
        x2_t = probs[:, :, :].rearrange("p r n -> p (r n)")[:, 2 * E * F:2 * E * F + 4 * S].rearrange(
            "p (r n) -> p r n", r=4)
        z_t = xin
        o_t = xn[:, :, :, :, :].rearrange("p a q k n -> p (a q k n)")[:, 0:2 * S].rearrange(
            "p (r q d) -> p r q d", r=2, q=QB)
        zst = sb("zst", [P, 2, QB, 6])
        zmv = sb("zmv", [P, 2, QB, 2])
        zrs = sb("zrs", [P, 2, 4, QB])

        ps_s = pb("ps_s", [P, 2, 512])
        ps_a = pb("ps_a", [P, 4, 512])
        ps_v = pb("ps_v", [P, 512])
        ps_m = pb("ps_m", [P, 512])

        QSTART = [0, P, 2 * P, 3 * P]
        PCOL = {0: 0, 1: 512, 3: 896, 2: 1024}

        PER = {"xT": 1, "qT": 1, "kT": 1, "v": 1, "mT": 4, "uT": 2, "aT": 1, "wo": 1, "nT": 1, "lg": 1, "rk": 1}
        MISC = {0: [("xT", 1, 0)], 1: [("mT", 0, 1)], 2: [("qT", 1, 0)], 3: [("kT", 1, 0)],
                4: [("v", 1, 0), ("nT", -2, 0)], 5: [("mT", 0, 2), ("lg", -2, 0)], 6: [("uT", -1, 1)],
                7: [("aT", -1, 0)], 9: [("mT", 0, 3)], 11: [("wo", -1, 0)], 12: [None, ("rk", -2, 0)],
                13: [("mT", 1, 0), ("uT", 0, 0)]}
        IN_TURN = [s for h in range(16) for s in MISC.get(h, []) if s]

        def ready(stage):
            return sem("ready_" + stage)

        def freed(stage):
            return sem("freed_" + stage)

        def iterations(eng, body, first=-1):
            for i in range(first, 3):
                body(At(i, i, False))
            with eng.Fori(3, NB - 4, 2) as r:
                body(At(r, 1, True))
                body(At(r + 1, 0, True))
            for i in range(NB - 3, NB + 3):
                body(At(i, i, False))

        def tiles(eng, body):
            for j in (0, 4):
                for t in range(4):
                    body(j, t)
            with eng.Fori(8, NT - 4, 4) as j:
                for t in range(4):
                    body(j, t)
            for t in range(4):
                body(NT - 4, t)

        def wait_from(eng, s, j, n):
            if isinstance(j, int) and j + n <= 0:
                return
            eng.wait_ge(s, j + n)

        def across(t, *shape):
            return t.unsqueeze(1).broadcast_to([P, *shape, t.shape[-1]])

        def along(t, n):
            return t.unsqueeze(len(t.shape)).broadcast_to([*t.shape, n])

        def place_max(sp, b, g):
            if not b.exists(NB):
                return
            need(sp, freed("mT"), 4, b, g + 1, sem("sp_passed"))
            for hl in range(2):
                sp.dma_start(qside[24 + hl:P:32, b.parity, g, :].bitcast(F32),
                             mt[GH * hl:GH * hl + GH, :]).then_inc(sem("max_placed"), 16)

        def place_side(sp, b, side, what, blocks, stage, done):
            need(sp, freed(stage), 1, b, 1, sem("sp_passed"))
            need(sp, sem(done), 16 * len(blocks) * GH + 32 * (what == 0), b, -(16 * len(blocks) * GH + 32 * (what == 0)), sem("sp_passed"))
            sp.dma_start(qk_d[b.parity, what], side[:, :, :].bitcast(F32)).then_inc(sem(done + "_d"), 16)
            need(sp, sem(done + "_d"), 16, b, 16, sem("sp_passed"))
            for r0, hl in blocks:
                for hp in range(GH):
                    of = qk_d[b.parity, what].rearrange("(g h d) s n -> h s d g n", h=GH, d=HD)[hp, hl]
                    if what == 0:
                        to = qside[32 * hp + r0:32 * hp + r0 + HD, b.parity, :, :]
                    else:
                        to = kside[32 * hp + r0:32 * hp + r0 + HD, b.parity, hp:NH:GH, :]
                    sp.dma_start(to.bitcast(F32), of).then_inc(sem(done), 16)

        def body_sp(sp, i):
            nxt, prev, ahead = i.plus(1), i.plus(-1), i.plus(2)
            if ahead.exists(NB):
                need(sp, sem("xbo_ready"), 1, i, 1, sem("sp_passed"))
                need(sp, ready("xT"), 1, i, 1, sem("sp_passed"))
                sp.dma_start(xin[:, ahead.parity], x_rows[bass.ds(ahead.value * S, S), :].rearrange(
                    "(i p) d -> p i d", p=P)).then_inc(sem(f"x_in{ahead.parity}"), 16)
            place_max(sp, i, 1)
            if nxt.exists(NB):
                if not i.loop and i.value < 1:
                    sp.wait_ge(sem(f"kside_ones{nxt.parity}"), 16 * 2 * GH)
                    sp.wait_ge(sem("qside_zero"), nxt.parity + 1)
                need(sp, sem("scores_ready"), UNITS, i, 0, sem("sp_passed"))
                for hl in range(2):
                    sp.dma_start(qside[24 + hl:P:32, nxt.parity, :, :].bitcast(F32),
                                 kside[26 + hl:P:32, nxt.parity, 0:GH, :].bitcast(F32)).then_inc(
                                     sem("q_placed"), 16)
                place_side(sp, nxt, qhl, 0, ((0, 0), (8, 0), (16, 1)), "qT", "q_placed")
                place_side(sp, nxt, khl, 1, ((0, 0), (8, 1), (16, 0)), "kT", "k_placed")
            place_max(sp, i, 2)
            if prev.plus(-1).exists(NB):
                b = prev.plus(-1)
                need(sp, sem("x2_ready"), 1, b, 1, sem("sp_passed"))
                sp.dma_start(x2_d[bass.ds(b.value * S, S), :].rearrange("(i p) d -> p i d", p=P),
                             x2[:, :, :]).then_inc(sem("x2_stored"), 16)
            if prev.exists(NB):
                need(sp, freed("aT"), 1, prev, 1, sem("sp_passed"))
                need(sp, sem("rows16_in"), 256, prev, 0, sem("sp_passed"))
                sp.dma_start(att_d, attt[:, :]).then_inc(sem("att_stored"), 16)
                need(sp, sem("att_stored"), 16, prev, 16, sem("sp_passed"))
                need(sp, ready("wo"), 1, prev, 0, sem("sp_passed"))
                for r in range(16):
                    of = att_d[:, 32 * r:32 * r + 32].rearrange("(h d) o -> d h o", d=HD)
                    sp.dma_start(rows16[HD * r:HD * r + HD, :].rearrange("d (h o) -> d h o", o=32),
                                 of).then_inc(sem("rows16_in"), 16)
            place_max(sp, i, 3)
            place_max(sp, nxt, 0)

        block = ctx.enter_context(nc.Block())

        @block.sync
        def _(sp):
            sp.dma_start(xin[:, 0], x_rows[0:S, :].rearrange("(i p) d -> p i d", p=P)).then_inc(sem("x_in0"), 16)
            for t, w in ((wq_s, wq), (wk_s, wk), (wv_s, wv)):
                for k in range(2):
                    for p2 in range(2):
                        n = (8 * k + 4 * p2) * HD
                        of = w[:, 64 * k:64 * k + 64].rearrange("r (j p d) -> r p j d", j=GH, p=2)[:, p2]
                        sp.dma_start(t[:, n:n + GH * HD].rearrange("r (j d) -> r j d", j=GH), of).then_inc(
                            sem("weights_in"), 16)
            sp.dma_start(wo_s[:], wo).then_inc(sem("weights_in"), 16)
            for t, w in ((bo_b, bo), (gam_b, gamma), (bet_b, beta)):
                sp.dma_start(t[:], w.unsqueeze(0).broadcast_to([P, D])).then_inc(sem("weights_in"), 16)
            sp.dma_start(wgt[:, :], wg.rearrange("e d -> d e"),
                         allow_slow_non_contiguous=True).then_inc(sem("weights_in"), 16)
            sp.dma_start(b1_r[:, :], b1.rearrange("e (c p) -> (e c) p", p=P)).then_inc(sem("weights_in"), 16)
            sp.wait_ge(sem("ones_ready"), 1)
            for par in range(2):
                sp.wait_ge(sem(f"kside_zero{par}"), 1)
                for hp in range(GH):
                    for half in range(2):
                        sp.dma_start(kside[32 * hp + 24:32 * hp + 26, par, hp + 8 * half:hp + 8 * half + 5:GH, :].bitcast(F32),
                                     w1_t[0:2, :, :]).then_inc(sem(f"kside_ones{par}"), 16)
                if par == 0:
                    body_sp(sp, At(-1, 1, False))
            sp.wait_ge(sem("zrow_ready"), 1)
            for e in range(E):
                sp.dma_start(rows_d[E * REG + e * P:E * REG + (e + 1) * P, :], zrow[:, :]).then_inc(
                    sem("pad_tiles"), 16)
            iterations(sp, lambda i: body_sp(sp, i), first=0)

            sp.wait_ge(sem("pv_done"), 4 * NB)
            sp.dma_start(w1_s, w1.rearrange("e p f -> p e f")).then_inc(sem("experts_in"), 16)
            sp.dma_start(b2_b, b2.unsqueeze(0).broadcast_to([P, E, D])).then_inc(sem("experts_in"), 16)
            for e in range(E):
                sp.dma_start(w2_s[:, e], w2[e].rearrange("(c p) d -> p c d", p=P)).then_inc(sem("experts_in"), 16)
            sp.wait_ge(sem("plan_ready"), 1)
            sp.wait_ge(sem("rows_sent"), 16 * (TOPK * QB * NB + E))
            sp.wait_ge(sem("pad_tiles"), 16 * E)

            def load_tile(j, t):
                row = sp.value_load(plan_i[0:1, 0, bass.ds(j + t, 1)], min_val=0, max_val=(E * REG + E * P - P))
                sp.dma_start(xs[:, t, :], rows_d[bass.ds(row, P), :]).then_inc(sem(f"tile_in{t}"), 16)

            for t in range(4):
                load_tile(0, t)
            with sp.Fori(4, NT - 3, 4) as j:
                for t in range(4):
                    wait_apart(sp, sem("sp_passed"), sem(f"sent{t}"), j * 4)
                    load_tile(j, t)
            for t in range(4):
                sp.wait_ge(sem(f"sent{t}"), 16 * (NT // 4))
            sp.wait_ge(sem("x2_stored"), 16 * NB)

            def load_last(b, r):
                sp.dma_start(y_t[:, r].rearrange("p (i n) -> p i n", i=QB),
                             y_d[bass.ds(b * (S * TOPK), S * TOPK), :].rearrange(
                                 "(i p k) d -> p i (k d)", p=P, k=TOPK)).then_inc(sem(f"y_in{r}"), 16)
                sp.dma_start(x2_t[:, r].rearrange("p (i n) -> p i n", i=QB),
                             x2_d[bass.ds(b * S, S), :].rearrange("(i p) d -> p i d", p=P)).then_inc(
                                 sem(f"y_in{r}"), 16)

            def store_last(b, r):
                wait_apart(sp, sem("sp_passed"), sem("o_ready"), b + 1)
                sp.dma_start(out_rows[bass.ds(b * S, S), :].rearrange("(i p) d -> p i d", p=P),
                             o_t[:, r % 2]).then_inc(sem(f"stored{r % 2}"), 16)

            for r in range(4):
                load_last(r, r)
            with sp.Fori(0, NB - 7, 4) as b:
                for r in range(4):
                    store_last(b + r, r)
                    wait_apart(sp, sem("sp_passed"), sem("z_done"), b + (r + 1))
                    load_last(b + (r + 4), r)
            for r in range(4):
                store_last(NB - 4 + r, r)
            for r in range(2):
                sp.wait_ge(sem(f"stored{r}"), 16 * (NB // 2))

        @block.gpsimd
        def _(pool):
            chain = [0]

            def link(ins):
                chain[0] += 1
                ins.then_inc(sem("pool_chain"), 1)
                pool.wait_ge(sem("pool_chain"), chain[0])

            pool.memset(ident[:], 0.0)
            pool.memset(identb[:], 0.0)
            pool.memset(onesb[:], 1.0)
            pool.memset(maskb[:], 0.0)
            pool.memset(halfneg[:], -0.5)
            link(pool.memset(lowerb[:], 0.0))
            for m in (ident, identb):
                pool.affine_select(out=m[:], in_=m[:], pattern=[[-1, P]], compare_op=ALU.not_equal, fill=1.0,
                                   base=0, channel_multiplier=1)
            pool.affine_select(out=maskb[:], in_=maskb[:], pattern=[[-1, P]], compare_op=ALU.is_ge, fill=NEG,
                               base=0, channel_multiplier=1)
            pool.affine_select(out=lowerb[:], in_=lowerb[:], pattern=[[-1, P]], compare_op=ALU.is_ge,
                               fill=1.0, base=0, channel_multiplier=1).then_inc(sem("consts"), 1)
            pool.memset(qside[:, 0].bitcast(F32), 0.0).then_inc(sem("qside_zero"), 1)
            pool.memset(vpad[:, 0], 0.0)
            link(pool.memset(vpad[:, 1], 0.0))
            vh = vpad[:, :, :, :, :].rearrange("p a b (k g j) c -> p (a b k) g j c", k=2, g=2)
            pool.memset(vh[:, :, 0, :, 8:16], 1.0)
            pool.memset(vh[:, :, 1, :, 24:32], 1.0).then_inc(sem("vpad_set"), 1)
            pool.iota(wtab_i[:], pattern=[[0, QB], [-1, E]], base=E, channel_multiplier=0)
            pool.iota(used_i[:], pattern=[[REG, E]], base=0, channel_multiplier=0)
            pool.iota(iotap[:], pattern=[[0, 1]], base=0, channel_multiplier=1)
            pool.iota(dest_i[:], pattern=[[TOPK * P, QB], [1, TOPK]], base=0, channel_multiplier=TOPK)
            pool.iota(tile_i[:], pattern=[[1, NT]], base=0, channel_multiplier=0)
            pool.memset(xn[:], 0.0)
            link(pool.memset(zrow[:], 0.0))
            pool.tensor_copy(wtab[:], wtab_i[:])
            pool.tensor_copy(used[:], used_i[:])
            pool.tensor_copy(first_row[:], used_i[:])
            pool.tensor_copy(iotapf[:], iotap[:])
            pool.tensor_copy(tile_f[:], tile_i[:])
            pool.tensor_copy(dest[:], dest_i[:])
            link(pool.memset(zrow[:, D:D + 1].bitcast(I32), SKIP))
            pool.memset(onehot[:], 0.0).then_inc(sem("zrow_ready"), 1)
            pool.memset(qside[:, 1].bitcast(F32), 0.0).then_inc(sem("qside_zero"), 1)
            pool.memset(kside[:, 1].bitcast(F32), 0.0).then_inc(sem("kside_zero1"), 1)

            def body(i):
                nxt, prev, late = i.plus(1), i.plus(-1), i.plus(-3)
                for h in range(NH):
                    if i.exists(NB):
                        need(pool, sem("exp_done"), UNITS, i, 3 * h + 2, sem("pool_passed"))
                        pr = probs[:, h % 8, :]
                        first = pr[:, 0:1024].rearrange("p (a n) -> p a n", a=2)[:, :, 0:P]
                        pool.affine_select(out=first, in_=first, pattern=[[0, 2], [1, P]],
                                           compare_op=ALU.is_ge, fill=0.0, base=0,
                                           channel_multiplier=-1).then_inc(sem("masked"), 1)
                        need(pool, sem("exp_done"), UNITS, i, 3 * h + 3, sem("pool_passed"))
                        last = pr[:, 896:1152].rearrange("p (a n) -> p a n", a=2)
                        pool.affine_select(out=last, in_=last, pattern=[[0, 2], [1, P]],
                                           compare_op=ALU.is_ge, fill=0.0, base=0,
                                           channel_multiplier=-1).then_inc(sem("masked"), 1)
                    if late.exists(NB) and 5 <= h <= 12:
                        q, k = (h - 5) // 2, (h - 5) % 2
                        if h == 5:
                            need(pool, sem("slot_ready"), 1, late, 1, sem("pool_passed"))
                            need(pool, sem("xn_ready"), 1, late, 1, sem("pool_passed"))
                        pool.indirect_dma_start(
                            rows_d, bass.IndirectOffsetOnAxis(ap=slot[:, late.parity, k, q:q + 1], axis=0),
                            xn[:, late.parity, q, k, :], None).then_inc(sem("rows_sent"), 16)
                    if nxt.exists(NB) and h == 12:
                        need(pool, freed("wo"), 1, prev, 1, sem("pool_passed"))
                        need(pool, sem(f"x_in{nxt.parity}"), 8, nxt, 16 - 8 * nxt.parity, sem("pool_passed"))
                        if not i.loop and i.value < 0:
                            pool.wait_ge(sem("weights_in"), 16 * WEIGHTS)
                        pool.tensor_tensor(xbo[:, nxt.parity], xin[:, nxt.parity], across(bo_b[:], QB),
                                           ALU.add).then_inc(sem("xbo_ready"), 1)
                    if prev.exists(NB):
                        if h == 13:
                            need(pool, sem("x1_ready"), 1, prev, 0, sem("pool_passed"))
                            rstd(pool, prev, 0)
                        if h == 15:
                            need(pool, sem("x1_ready"), 1, prev, 1, sem("pool_passed"))
                            need(pool, sem("x2_stored"), 16, prev, 0, sem("pool_passed"))
                            pool.tensor_scalar(x2[:], x1[:], 2.0, None, ALU.mult).then_inc(sem("x2_ready"), 1)
                            need(pool, sem("xc_ready"), 1, prev, 0, sem("pool_passed"))
                            rstd(pool, prev, 1)
                    if prev.plus(-1).exists(NB) and h == 1:
                        make_rows(pool, prev.plus(-1))

            def rstd(pool, b, which):
                need(pool, sem(f"var{which}"), 1, b, 1, sem("pool_passed"))
                v, r, s, t = (rs[:, which, k, :] for k in range(4))
                for k, step in enumerate((
                        lambda: pool.tensor_scalar(v, mv[:, which, :, 1], EPS, None, ALU.add),
                        lambda: pool.tensor_tensor(r, v, halfneg[:], ALU.pow),
                        lambda: pool.tensor_tensor(s, r, r, ALU.mult),
                        lambda: pool.tensor_tensor(s, s, v, ALU.mult),
                        lambda: pool.tensor_scalar(s, s, -0.5, 1.5, ALU.mult, ALU.add),
                        lambda: pool.tensor_tensor(t, r, s, ALU.mult))):
                    if k:
                        need(pool, sem(f"rstd{which}"), 6, b, k, sem("pool_passed"))
                    step().then_inc(sem(f"rstd{which}"), 1)

            def make_rows(pool, b):
                need(pool, sem("xc_ready"), 1, b, 1, sem("pool_passed"))
                need(pool, sem("rows_sent"), 16 * TOPK * QB, b.plus(-1), 0, sem("pool_passed"))
                need(pool, ready("nT"), 1, b.plus(-1), 0, sem("pool_passed"))
                pool.tensor_tensor(xc[:], xc[:], across(gam_b[:], QB), ALU.mult).then_inc(sem("xn_steps"), 1)
                pool.tensor_copy(xn[:, b.parity, :, :, D].bitcast(I32), dest[:]).then_inc(sem("xn_steps"), 1)
                need(pool, sem("xn_steps"), 4, b, 2, sem("pool_passed"))
                pool.tensor_tensor(xn[:, b.parity, :, 0, 0:D], xc[:], across(bet_b[:], QB),
                                   ALU.add).then_inc(sem("xn_steps"), 1)
                pool.tensor_scalar(dest[:], dest[:], float(TOPK * S), None, ALU.add).then_inc(sem("xn_steps"), 1)
                need(pool, sem("xn_steps"), 4, b, 4, sem("pool_passed"))
                pool.tensor_copy(xn[:, b.parity, :, 1, 0:D], xn[:, b.parity, :, 0, 0:D]).then_inc(sem("xn_ready"), 1)

            iterations(pool, body)

            pool.wait_ge(sem("route"), ROUTE * NB)
            link(pool.tensor_tensor(padf[:], used[:], iotapf[:].broadcast_to([P, E]), ALU.add))
            link(pool.tensor_copy(padix[:], padf[:]))
            for e in range(E):
                pool.indirect_dma_start(rows_d, bass.IndirectOffsetOnAxis(ap=padix[:, e:e + 1], axis=0),
                                        zrow[:], None).then_inc(sem("rows_sent"), 16)

            def send(j, t):
                wait_apart(pool, sem("pool_passed"), sem("ys_ready"), j + (t + 1))
                pool.indirect_dma_start(
                    y_d, bass.IndirectOffsetOnAxis(ap=xs[:, t, D:D + 1].bitcast(I32), axis=0), ys[:, t, :], None,
                    bounds_check=T * TOPK - 1, oob_is_err=False).then_inc(sem(f"sent{t}"), 16)

            tiles(pool, send)

            def zrstd(b, r):
                wait_apart(pool, sem("pool_passed"), sem("zvar"), b + (r + 1))
                v, s, u, t = (zrs[:, r % 2, k, :] for k in range(4))
                for k, step in enumerate((
                        lambda: pool.tensor_scalar(v, zmv[:, r % 2, :, 1], EPS, None, ALU.add),
                        lambda: pool.tensor_tensor(s, v, halfneg[:], ALU.pow),
                        lambda: pool.tensor_tensor(u, s, s, ALU.mult),
                        lambda: pool.tensor_tensor(u, u, v, ALU.mult),
                        lambda: pool.tensor_scalar(u, u, -0.5, 1.5, ALU.mult, ALU.add),
                        lambda: pool.tensor_tensor(t, s, u, ALU.mult))):
                    if k:
                        wait_apart(pool, sem("pool_passed"), sem("zrstd"), b * 6 + (6 * r + k))
                    step().then_inc(sem("zrstd"), 1)

            with pool.Fori(0, NB - 3, 4) as b:
                for r in range(4):
                    zrstd(b, r)

        @block.scalar
        def _(act):
            def body(i):
                nxt, prev, rb = i.plus(1), i.plus(-1), i.plus(-2)
                for h in range(NH):
                    if h == 4 and prev.exists(NB):
                        copy_u(act, prev, 1)
                    if h == 12 and i.exists(NB):
                        copy_u(act, i, 0)
                    for u in range(3):
                        if i.exists(NB):
                            if h % 4 == 0 and u == 0:
                                need(act, sem("pv_done"), 4, i, h // 4 - 1)
                            n = 3 * h + u
                            need(act, sem("scores_ready"), UNITS, i, n + 1)
                            c0, to = ((0, 0), (P, 512), (P, 896))[u]
                            nc.scalar.activation(probs[:, h % 8, to:to + 512 - c0], ps_s[:, n % 2, c0:512],
                                                 ACT.Exp, scale=SCALE).then_inc(sem("exp_done"), 1)
                        if u == 1:
                            middle(act, h, i, nxt, prev, rb)

            def copy_u(act, b, k):
                need(act, sem("pv_done"), 4, b, 2 * k + 2)
                need(act, ready("uT"), 2, b, k)
                nc.scalar.activation(ucp[:], ps_v[:], ACT.Copy).then_inc(sem("u_copied"), 1)

            def middle(act, h, i, nxt, prev, rb):
                if nxt.exists(NB):
                    if h == 0:
                        need(act, ready("xT"), 1, nxt, 1)
                        need(act, ready("v"), 1, nxt, 0)
                        nc.scalar.activation(xt[:], ps_m[:], ACT.Copy).then_inc(freed("xT"), 1)
                    if h == 2:
                        need(act, ready("qT"), 1, nxt, 1)
                        need(act, sem("q_placed_d"), 16, nxt, 0)
                        nc.scalar.activation(qhl[:, 0], ps_m[:], ACT.Copy).then_inc(sem("q_high"), 1)
                    if h == 3:
                        need(act, ready("kT"), 1, nxt, 1)
                        need(act, sem("k_placed_d"), 16, nxt, 0)
                        nc.scalar.activation(khl[:, 0], ps_m[:], ACT.Copy).then_inc(sem("k_high"), 1)
                if rb.exists(NB):
                    if h == 5:
                        need(act, ready("nT"), 1, rb, 1)
                        need(act, ready("lg"), 1, rb, 0)
                        nc.scalar.activation(xnt[:], ps_m[:], ACT.Copy).then_inc(freed("nT"), 1)
                    if h == 8:
                        need(act, sem("route"), ROUTE, rb, 2)
                        nc.scalar.activation(rt[:, 2], rt[:, 1], ACT.Exp).then_inc(sem("gate_exp"), 1)
                    if h == 11:
                        need(act, sem("route"), ROUTE, rb, 8)
                        nc.scalar.activation(rv[:, 4], rv[:, 3], ACT.Exp).then_inc(sem("gate_exp"), 1)
                if prev.exists(NB):
                    if h == 7:
                        need(act, ready("aT"), 1, prev, 1)
                        need(act, sem("att_stored"), 16, prev, 0)
                        nc.scalar.activation(attt[:].rearrange("p (r o) -> p o r", r=16),
                                             ps_m[:].rearrange("p (o r) -> p o r", r=16),
                                             ACT.Copy).then_inc(freed("aT"), 1)

            iterations(act, body)

            act.wait_ge(sem("plan_ready"), 1)
            act.wait_ge(sem("b1_ready"), 1)

            def hidden(j, t):
                e = act.value_load(plan_i[0:1, 1, bass.ds(j + t, 1)], min_val=0, max_val=E - 1)
                act.wait_ge(sem("h_ready"), j + (t + 1))
                wait_from(act, sem("y_ready"), j, t - 1)
                for c in range(FC):
                    ins = nc.scalar.activation(ht[:, t % 2, c, :], ps_a[:, t % 2, c * P:(c + 1) * P],
                                               ACT.Gelu_apprx_tanh,
                                               bias=b1_s[:, bass.ds(e, 1), c:c + 1].rearrange("p a b -> p (a b)"))
                ins.then_inc(sem("ht_ready"), 1)

            tiles(act, hidden)

        @block.tensor
        def _(pe):
            turn = {}

            def misc(i, name, off, place):
                b = i.plus(off)
                if not b.exists(NB):
                    return
                at = IN_TURN.index((name, off, place))
                for back in range(1, len(IN_TURN)):
                    n2, off2, place2 = IN_TURN[(at - back) % len(IN_TURN)]
                    b2_ = i.plus(off2 - (1 if at - back < 0 else 0))
                    if b2_.exists(NB):
                        if n2 == "rk":
                            need(pe, sem("route"), ROUTE, b2_, 14)
                        else:
                            need(pe, freed(n2), PER[n2], b2_, place2 + 1)
                        break
                stages[name](b, place).then_inc(ready(name), 1)

            def tr(src):
                for q in range(QB):
                    ins = pe.transpose(ps_m[:, q * P:(q + 1) * P], src(q), ident[:])
                return ins

            def st_xT(b, place):
                need(pe, sem(f"x_in{b.parity}"), 8, b, 16 - 8 * b.parity)
                return tr(lambda q: xin[:, b.parity, q, :])

            def st_qT(b, place):
                need(pe, freed("xT"), 1, b, 1)
                if not b.loop and b.value == 0:
                    pe.wait_ge(sem("weights_in"), 16 * WEIGHTS)
                return pe.matmul(ps_m[:], wq_s[:], xt[:], start=True, stop=True)

            def st_kT(b, place):
                return pe.matmul(ps_m[:], wk_s[:], xt[:], start=True, stop=True)

            def st_v(b, place):
                for q in range(QB):
                    ins = pe.matmul(ps_m[:, q * P:(q + 1) * P], xt[:, q * P:(q + 1) * P], wv_s[:],
                                    start=True, stop=True)
                return ins

            def st_mT(b, g):
                need(pe, sem("max_split"), 8, b, 2 * g + 2)
                for q in range(QB):
                    ins = pe.transpose(ps_m[0:2 * GH, q * P:(q + 1) * P],
                                       mhl[:, q].bitcast(F32).rearrange("p a b -> p (a b)"), ident[:])
                return ins

            def st_uT(b, k):
                need(pe, sem("u_copied"), 2, b, k + 1)
                return tr(lambda q: ucp[:, q * P:(q + 1) * P])

            def st_aT(b, place):
                need(pe, freed("uT"), 2, b, 2)
                return tr(lambda q: att[:, q, :])

            def st_wo(b, place):
                need(pe, sem("rows16_in"), 256, b, 256)
                for q in range(QB):
                    ins = pe.matmul(ps_m[:, q * P:(q + 1) * P], rows16[:, q * P:(q + 1) * P], wo_s[:],
                                    start=True, stop=True)
                return ins

            def st_nT(b, place):
                need(pe, sem("xn_ready"), 1, b, 1)
                return tr(lambda q: xn[:, b.parity, q, 0, 0:D])

            def st_lg(b, place):
                need(pe, freed("nT"), 1, b, 1)
                for q in range(QB):
                    ins = pe.matmul(ps_m[:, q * E:(q + 1) * E], xnt[:, q * P:(q + 1) * P], wgt[:],
                                    start=True, stop=True)
                return ins

            def st_rk(b, place):
                need(pe, sem("route"), ROUTE, b, 12)
                n = (QB + 1) * E
                pe.matmul(ps_m[:, 0:n], lowerb[:], onehot[:].rearrange("p a e -> p (a e)"), start=True, stop=False)
                for s in range(QB):
                    ins = pe.matmul(ps_m[:, (s + 1) * E:n].rearrange("p (a e) -> p a e", e=E), onesb[:],
                                    across(onehot[:, s, :], QB - s), start=False, stop=(s == QB - 1))
                return ins

            stages = dict(xT=st_xT, qT=st_qT, kT=st_kT, v=st_v, mT=st_mT, uT=st_uT, aT=st_aT, wo=st_wo,
                          nT=st_nT, lg=st_lg, rk=st_rk)

            def scores(i, h, u):
                if not i.exists(NB):
                    return
                g, n = h // GH, 3 * h + u
                if h % GH == 0 and u == 0:
                    need(pe, sem("max_placed"), 32 * 4, i, 32 * (g + 1))
                need(pe, sem("exp_done"), UNITS, i, n - 1)
                for kb, q0, c0 in (((0, 0, 0),), ((1, P, P),), ((3, 2 * P, 0), (2, 2 * P, 2 * P)))[u]:
                    ins = pe.matmul(ps_s[:, n % 2, c0:c0 + S - q0], kside[:, i.parity, h, kb * P:(kb + 1) * P],
                                    qside[:, i.parity, g, q0:S], start=True, stop=True)
                ins.then_inc(sem("scores_ready"), 1)

            def maxima(b, n):
                if not b.exists(NB):
                    return
                if n == 0:
                    need(pe, sem("q_placed"), 16 * 14, b, 16 * 14)
                    need(pe, sem("k_placed"), 16 * 12, b, 16 * 12)
                need(pe, sem("max_taken"), AUNITS, b, n - 1)
                for s in range(2):
                    h = 2 * (n // 3) + s
                    to = ps_a[:, 2 * (n % 2) + s, :]
                    for qb, nk, c0 in (((3, S, 0),), ((2, 3 * P, 0),), ((0, 2 * P, 0), (1, 2 * P, 2 * P)))[n % 3]:
                        pe.matmul(to[:, c0:c0 + nk], qside[:, b.parity, h // GH, qb * P:(qb + 1) * P],
                                  kside[:, b.parity, h, 0:nk], start=True, stop=False)
                        c1 = c0 + qb * P
                        ins = pe.matmul(to[:, c1:c1 + P], identb[:], maskb[:], start=False, stop=True)
                ins.then_inc(sem("max_scores"), 1)

            def values(b, g, kbs):
                if not b.exists(NB):
                    return
                if kbs[0] == 0:
                    need(pe, sem("masked"), 2 * NH, b, 2 * GH * (g + 1))
                    if g == 0:
                        need(pe, freed("v"), 1, b, 1)
                    if g % 2 == 0:
                        need(pe, sem("u_copied"), 2, b, g // 2)
                for kb in kbs:
                    for j in range(GH):
                        h = GH * g + j
                        c = PCOL[kb]
                        ins = pe.matmul(ps_v[32 * j:32 * j + 32, kb * P:S], vpad[:, b.parity, kb, h, :],
                                        probs[:, h % 8, c:c + S - kb * P],
                                        start=(g % 2 == 0 and kb == 0), stop=(g % 2 == 1 and kb == kbs[-1] == 2),
                                        skip_group_check=True)
                if kbs[-1] == 2:
                    ins.then_inc(sem("pv_done"), 1)

            pe.wait_ge(sem("consts"), 1)

            def body(i):
                for h in range(NH):
                    mb, mg = (i, h // 4 + 2) if h < 8 else (i.plus(1), h // 4 - 2)
                    mu = 6 * mg + 3 * (h % 4 // 2)
                    scores(i, h, 0)
                    maxima(mb, mu + (2 if h % 2 else 0))
                    scores(i, h, 1)
                    stages_here = MISC.get(h, [])
                    if stages_here and stages_here[0]:
                        misc(i, *stages_here[0])
                    if h % 2 == 0:
                        maxima(mb, mu + 1)
                    scores(i, h, 2)
                    if h % 4:
                        vb, vg = (i, h // 4 - 1) if h >= 4 else (i.plus(-1), 3)
                        values(vb, vg, ((0,), (1,), (3, 2))[h % 4 - 1])
                    for s in stages_here[1:]:
                        misc(i, *s)

            iterations(pe, body)

            pe.wait_ge(sem("weights_in"), 16 * WEIGHTS)
            pe.wait_ge(sem("route"), ROUTE * NB)
            pe.transpose(ps_m[:, 0:E * FC], b1_r[:, :], ident[0:E * FC, 0:E * FC]).then_inc(sem("b1_turned"), 1)
            pe.wait_ge(sem("b1_ready"), 1)
            pe.wait_ge(sem("plan_ready"), 1)
            pe.wait_ge(sem("experts_in"), 16 * (E + 2))

            def turn_tile(j, t):
                pe.wait_ge(sem(f"tile_in{t % 4}"), j * 4 + 16 * (t // 4 + 1))
                wait_from(pe, sem("xst_ready"), j, t - 1)
                to = (ps_m, ps_v)[t % 2]
                pe.transpose(to[:, 0:P], xs[:, t % 4, 0:D], ident[:]).then_inc(sem("tile_turned"), 1)

            def first_product(j, t):
                pe.wait_ge(sem("xst_ready"), j + (t + 1))
                pe.wait_ge(sem("w1_ready"), j + (t + 1))
                wait_from(pe, sem("ht_ready"), j, t - 1)
                for c in range(FC):
                    ins = pe.matmul(ps_a[:, t % 2, c * P:(c + 1) * P], w1_t[:, t % 2, c * P:(c + 1) * P],
                                    xst[:, t % 2, :], start=True, stop=True)
                ins.then_inc(sem("h_ready"), 1)

            def second_product(j, t):
                e = pe.value_load(plan_i[0:1, 1, bass.ds(j + t, 1)], min_val=0, max_val=E - 1)
                pe.wait_ge(sem("ht_ready"), j + (t + 1))
                wait_from(pe, sem("ys_ready"), j, t - 1)
                for c in range(FC):
                    ins = pe.matmul(ps_s[:, t % 2, 0:D], ht[:, t % 2, c, :],
                                    w2_s[:, bass.ds(e, 1), c, :].rearrange("p a d -> p (a d)"),
                                    start=(c == 0), stop=(c == FC - 1))
                ins.then_inc(sem("y_ready"), 1)

            def tile(j, t):
                last = isinstance(j, int) and j + t == NT - 1
                if not last:
                    turn_tile(j, t + 1)
                first_product(j, t)
                if not (isinstance(j, int) and j + t == 0):
                    second_product(j, t - 1)
                if last:
                    second_product(j, t)

            turn_tile(0, 0)
            tiles(pe, tile)

        @block.vector
        def _(dve):
            dve.memset(kside[:, 0].bitcast(F32), 0.0).then_inc(sem("kside_zero0"), 1)
            dve.memset(w1_t[0:2, :, :], 1.0).then_inc(sem("ones_ready"), 1)
            dve.wait_ge(sem("zrow_ready"), 1)

            def maximum(b, n, part):
                if not b.exists(NB):
                    return
                need(dve, sem("max_scores"), AUNITS, b, n + 1)
                qb, nk, c0 = (((3, S, 0),), ((2, 3 * P, 0),), ((1, 2 * P, 2 * P), (0, P, 0)))[n % 3][part]
                s = 2 * (n // 3 % 2)
                ins = nc.vector.tensor_reduce(
                    negmax[:, n // 6 % 2, qb, s:s + 2], ps_a[:, 2 * (n % 2):2 * (n % 2) + 2, c0:c0 + nk], AX.X, ALU.max,
                    negate=True)
                if n % 3 < 2 or part == 1:
                    ins.then_inc(sem("max_taken"), 1)

            def split_max(b, g, low):
                if not b.exists(NB):
                    return
                if not low:
                    need(dve, sem("max_taken"), AUNITS, b, 6 * (g + 1))
                    need(dve, ready("mT"), 4, b, g)
                    nc.vector.tensor_copy(mhl[:, :, 0, :], negmax[:, g % 2]).then_inc(sem("max_split"), 1)
                else:
                    need(dve, sem("max_split"), 8, b, 2 * g + 1)
                    nc.vector.tensor_tensor(mhl[:, :, 1, :], negmax[:, g % 2], mhl[:, :, 0, :].bitcast(F32),
                                            ALU.subtract).then_inc(sem("max_split"), 1)

            def copy_max(b, g):
                if not b.exists(NB):
                    return
                need(dve, ready("mT"), 4, b, g + 1)
                need(dve, sem("max_placed"), 128, b, 32 * g)
                nc.vector.tensor_copy(mt[:], ps_m[0:2 * GH, :]).then_inc(freed("mT"), 1)

            def low_part(b, side, name, high, stage):
                need(dve, sem(high), 1, b, 1)
                nc.vector.tensor_tensor(side[:, 1], ps_m[:], side[:, 0].bitcast(F32),
                                        ALU.subtract).then_inc(freed(stage), 1)

            def copy_v(b):
                need(dve, ready("v"), 1, b, 1)
                need(dve, sem("pv_done"), 4, b.plus(-1), 0)
                if not b.loop and b.value == 0:
                    dve.wait_ge(sem("vpad_set"), 1)
                of = ps_m[:].rearrange("p (a g j d) -> p a g j d", a=2 * QB, g=2, j=GH)
                to = vpad[:, b.parity].rearrange("p b (k g j) c -> p (b k) g j c", k=2, g=2)
                nc.vector.tensor_copy(to[:, :, 0, :, 0:HD], of[:, :, 0])
                nc.vector.tensor_copy(to[:, :, 1, :, 16:16 + HD], of[:, :, 1]).then_inc(freed("v"), 1)

            def divide(b, k, second):
                of = ps_m[:].rearrange("p (q a c) -> p q a c", q=QB, c=16)
                if not second:
                    need(dve, ready("uT"), 2, b, k + 1)
                    nc.vector.reciprocal(urec[:], of[:, :, :, 8]).then_inc(sem("recip"), 1)
                else:
                    need(dve, sem("recip"), 2, b, k + 1)
                    need(dve, ready("aT"), 1, b, 0)
                    nc.vector.tensor_tensor(att[:, :, 64 * k:64 * k + 64].rearrange("p q (a d) -> p q a d", d=HD),
                                            of[:, :, :, 0:HD], along(urec[:], HD), ALU.mult).then_inc(freed("uT"), 1)

            def statistics(b, which, src):
                for q in range(QB):
                    ins = nc.vector.bn_stats(stats[:, which, q, :], src[:, q, :])
                ins.then_inc(sem("stats"), 1)

            def aggregate(b, which):
                need(dve, sem("stats"), 2, b, which + 1, sem("dve_passed"))
                for q in range(QB):
                    ins = nc.vector.bn_aggr(mv[:, which, q, :], stats[:, which, q, :])
                ins.then_inc(sem(f"var{which}"), 1)

            def normalize(b, which, dst, src, done):
                need(dve, sem(f"rstd{which}"), 6, b, 6)
                for q in range(QB):
                    ins = nc.vector.tensor_scalar(dst[:, q, :], src[:, q, :], mv[:, which, q, 0:1],
                                                  rs[:, which, 3, q:q + 1], ALU.subtract, ALU.mult)
                ins.then_inc(sem(done), 1)

            V = nc.vector
            best, d_best, z, e2, c1, v2, c2 = (rv[:, k] for k in (0, 3, 6, 4, 1, 2, 5))
            eq1, diff, ex, w1c, m1, rest, eq2, w2c, m2, place, p1, p2 = (rt[:, k] for k in range(12))

            def g(b, k):
                return gates[:, bass.ds(b.value * QB, QB), k]

            ROUTING = [
                lambda b: [V.tensor_reduce(best, lg[:], AX.X, ALU.max)],
                lambda b: [V.tensor_tensor(eq1, lg[:], along(best, E), ALU.is_equal),
                           V.tensor_tensor(diff, lg[:], along(best, E), ALU.subtract)],
                lambda b: [V.tensor_tensor(w1c, eq1, wtab[:], ALU.mult)],
                lambda b: [V.tensor_reduce(c1, w1c, AX.X, ALU.max)],
                lambda b: [V.tensor_tensor(m1, wtab[:], along(c1, E), ALU.is_equal)],
                lambda b: [V.scalar_tensor_tensor(out=rest, in0=m1, scalar=NEG, in1=lg[:], op0=ALU.mult,
                                                  op1=ALU.add)],
                lambda b: [V.tensor_reduce(v2, rest, AX.X, ALU.max)],
                lambda b: [V.tensor_tensor(eq2, rest, along(v2, E), ALU.is_equal),
                           V.tensor_tensor(d_best, v2, best, ALU.subtract)],
                lambda b: [V.tensor_tensor(w2c, eq2, wtab[:], ALU.mult)],
                lambda b: [V.tensor_reduce(c2, w2c, AX.X, ALU.max)],
                lambda b: [V.tensor_tensor(m2, wtab[:], along(c2, E), ALU.is_equal)],
                lambda b: [V.tensor_tensor(onehot[:, 0:QB, :], m1, m2, ALU.add)],
                lambda b: [V.tensor_tensor(place, ps_m[:, 0:QB * E].rearrange("p (q e) -> p q e", e=E),
                                           across(used[:], QB), ALU.add)],
                lambda b: [V.tensor_tensor(used[:], ps_m[:, QB * E:(QB + 1) * E], used[:], ALU.add)],
                lambda b: [V.tensor_tensor(p1, m1, place, ALU.mult), V.tensor_tensor(p2, m2, place, ALU.mult)],
                lambda b: [V.tensor_reduce(z, ex, AX.X, ALU.add)],
                lambda b: [V.scalar_tensor_tensor(out=z, in0=z, scalar=1e-9, in1=e2, op0=ALU.mult, op1=ALU.add)],
                lambda b: [V.tensor_scalar(z, z, 1.0, None, ALU.add)],
                lambda b: [V.reciprocal(g(b, 0), z)],
                lambda b: [V.tensor_tensor(g(b, 1), e2, g(b, 0), ALU.mult)],
            ]
            assert len(ROUTING) == ROUTE

            def route(b, n):
                if not b.exists(NB):
                    return
                need(dve, sem("route"), ROUTE, b, n)
                if n == 0:
                    need(dve, freed("lg"), 1, b, 1)
                if n == 1:
                    need(dve, sem("gate_exp"), 2, b, 0)
                if n == 11:
                    need(dve, ready("rk"), 1, b, 0)
                if n == 15:
                    need(dve, sem("gate_exp"), 2, b, 1)
                if n == 16:
                    need(dve, sem("gate_exp"), 2, b, 2)
                if n == 12:
                    need(dve, ready("rk"), 1, b, 1)
                ROUTING[n](b)[-1].then_inc(sem("route"), 1)

            def rows_of(b):
                if not b.exists(NB):
                    return
                need(dve, sem("route"), ROUTE, b, 15)
                with nc.allow_low_precision(reason="row numbers, whole and under 2**24"):
                    V.tensor_reduce(slot[:, b.parity, 0], p1, AX.X, ALU.add)
                    V.tensor_reduce(slot[:, b.parity, 1], p2, AX.X, ALU.add).then_inc(sem("slot_ready"), 1)

            def body(i):
                nxt, prev, rb = i.plus(1), i.plus(-1), i.plus(-2)
                for h in range(NH):
                    mb, mg = (i, h // 4 + 2) if h < 8 else (i.plus(1), h // 4 - 2)
                    mu = 6 * mg + 3 * (h % 4 // 2)
                    gb, gg = ((i, 1), (i, 2), (i, 3), (nxt, 0))[h // 4]
                    for half in range(2):
                        if h % 2 == 0:
                            maximum(mb, mu + half, 0)
                        else:
                            maximum(mb, mu + 2, half)
                        at = 2 * h + half
                        if h % 4 == 0:
                            split_max(gb, gg, half)
                        if h % 4 == 1 and half:
                            copy_max(gb, gg)
                        if 13 <= at <= 24:
                            route(rb, at - 13)
                        if at == 26:
                            route(rb, 12)
                            route(rb, 13)
                        if at == 28:
                            route(rb, 14)
                        if at == 29:
                            rows_of(rb)
                        if at < 5:
                            route(i.plus(-3), 15 + at)
                        if nxt.exists(NB):
                            if at == 5:
                                low_part(nxt, qhl, "q", "q_high", "qT")
                            if at == 7:
                                low_part(nxt, khl, "k", "k_high", "kT")
                            if at == 9:
                                copy_v(nxt)
                        if prev.exists(NB):
                            if at in (13, 14):
                                divide(prev, 1, at == 14)
                            if at == 23:
                                need(dve, ready("wo"), 1, prev, 1)
                                need(dve, sem("xbo_ready"), 1, prev, 1)
                                V.tensor_tensor(ysum[:], ps_m[:].rearrange("p (q d) -> p q d", q=QB),
                                                xbo[:, prev.parity], ALU.add).then_inc(freed("wo"), 1)
                            if at == 24:
                                need(dve, freed("wo"), 1, prev, 1)
                                statistics(prev, 0, ysum)
                            if at == 25:
                                aggregate(prev, 0)
                            if at == 28:
                                need(dve, sem("x2_ready"), 1, prev, 0)
                                normalize(prev, 0, x1, ysum, "x1_ready")
                            if at == 29:
                                need(dve, sem("x1_ready"), 1, prev, 1)
                                statistics(prev, 1, x1)
                            if at == 30:
                                aggregate(prev, 1)
                        if rb.exists(NB):
                            if at == 1:
                                need(dve, sem("xn_ready"), 1, rb, 0)
                                normalize(rb, 1, xc, x1, "xc_ready")
                            if at == 12:
                                need(dve, ready("lg"), 1, rb, 1)
                                V.tensor_copy(lg[:], ps_m[:, 0:QB * E].rearrange("p (q e) -> p q e", e=E)).then_inc(
                                    freed("lg"), 1)
                        if i.exists(NB) and at in (27, 28):
                            divide(i, 0, at == 28)

            iterations(dve, body)

            step = [0]

            def link(ins):
                step[0] += 1
                ins.then_inc(sem("plan_steps"), 1)
                dve.wait_ge(sem("plan_steps"), step[0])

            c, whole, coef, ends, ones8 = (cnt[:, k] for k in range(5))
            dve.wait_ge(sem("route"), ROUTE * NB)
            V.memset(ones8, 1.0)
            link(V.tensor_tensor(c, used[0:1, :], first_row[0:1, :], ALU.subtract))
            link(V.tensor_scalar(c, c, float(P - 1), None, ALU.add))
            link(V.tensor_copy(cnt_i[:, 0], c))
            link(V.tensor_scalar(cnt_i[:, 1], cnt_i[:, 0], 7, None, ALU.arith_shift_right))
            link(V.tensor_copy(whole, cnt_i[:, 1]))
            V.tensor_scalar(coef, whole, -float(P), float(REG), ALU.mult, ALU.add)
            link(V.tensor_tensor_scan(ends, ones8, whole, 0.0, ALU.mult, ALU.add))
            expert, row, past = (plan[:, k] for k in range(3))
            V.memset(expert, 0.0)
            link(V.tensor_scalar(row, tile_f[0:1, :], float(P), None, ALU.mult))
            for e in range(E):
                V.tensor_scalar(past, tile_f[0:1, :], ends[:, e:e + 1], coef[:, e:e + 1], ALU.is_ge, ALU.mult)
                link(V.scalar_tensor_tensor(out=expert, in0=tile_f[0:1, :], scalar=ends[:, e:e + 1], in1=expert,
                                            op0=ALU.is_ge, op1=ALU.add))
                link(V.tensor_tensor(row, row, past, ALU.add))
            link(V.tensor_scalar(expert, expert, float(E - 1), None, ALU.min))
            V.tensor_copy(plan_i[:, 0], row)
            V.tensor_copy(plan_i[:, 1], expert).then_inc(sem("plan_ready"), 1)

            dve.wait_ge(sem("b1_turned"), 1)
            V.tensor_copy(b1_s[:].rearrange("p e c -> p (e c)"), ps_m[:, 0:E * FC]).then_inc(sem("b1_ready"), 1)
            dve.wait_ge(sem("plan_ready"), 1)
            dve.wait_ge(sem("experts_in"), 16 * (E + 2))

            def weights(j, t):
                e = dve.value_load(plan_i[0:1, 1, bass.ds(j + t, 1)], min_val=0, max_val=E - 1)
                wait_from(dve, sem("h_ready"), j, t - 1)
                V.tensor_copy(w1_t[:, t % 2, :],
                              w1_s[:, bass.ds(e, 1), :].rearrange("p a f -> p (a f)")).then_inc(sem("w1_ready"), 1)

            def turned(j, t):
                dve.wait_ge(sem("tile_turned"), j + (t + 1))
                wait_from(dve, sem("h_ready"), j, t - 1)
                V.tensor_copy(xst[:, t % 2, :], (ps_m, ps_v)[t % 2][:, 0:P]).then_inc(sem("xst_ready"), 1)

            def result(j, t):
                e = dve.value_load(plan_i[0:1, 1, bass.ds(j + t, 1)], min_val=0, max_val=E - 1)
                dve.wait_ge(sem("y_ready"), j + (t + 1))
                before = j * 4 + 16 * (t // 4)
                if not (isinstance(j, int) and before <= 0):
                    dve.wait_ge(sem(f"sent{t % 4}"), before)
                V.tensor_tensor(ys[:, t % 4, :], ps_s[:, t % 2, 0:D],
                                b2_b[:, bass.ds(e, 1), :].rearrange("p a d -> p (a d)"),
                                ALU.add).then_inc(sem("ys_ready"), 1)

            def tile(j, t):
                last = isinstance(j, int) and j + t == NT - 1
                if not last:
                    weights(j, t + 1)
                    turned(j, t + 1)
                if not (isinstance(j, int) and j + t == 0):
                    result(j, t - 1)
                if last:
                    result(j, t)

            weights(0, 0)
            turned(0, 0)
            tiles(dve, tile)

            def last_sum(b, r):
                dve.wait_ge(sem(f"y_in{r}"), b * 8 + 32)
                if not (isinstance(b, int) and b + r < 2):
                    dve.wait_ge(sem("o_ready"), b + (r - 1))
                yt = y_t[:, r].rearrange("p (q k d) -> p q k d", q=QB, k=TOPK)
                xt2 = x2_t[:, r].rearrange("p (q d) -> p q d", q=QB)
                for k in range(TOPK):
                    for q in range(QB):
                        gate = gates[:, bass.ds(b * QB + (r * QB + q), 1), k]
                        ins = V.scalar_tensor_tensor(out=z_t[:, r % 2, q, :], in0=yt[:, q, k, :], scalar=gate,
                                                     in1=z_t[:, r % 2, q, :] if k else xt2[:, q, :],
                                                     op0=ALU.mult, op1=ALU.add)
                    if k == 0:
                        ins.then_inc(sem("z_half"), 1)
                        dve.wait_ge(sem("z_half"), b + (r + 1))
                ins.then_inc(sem("z_done"), 1)
                dve.wait_ge(sem("z_done"), b + (r + 1))
                for q in range(QB):
                    ins = V.bn_stats(zst[:, r % 2, q, :], z_t[:, r % 2, q, :])
                ins.then_inc(sem("zstats"), 1)
                wait_apart(dve, sem("dve_passed"), sem("zstats"), b + (r + 1))
                for q in range(QB):
                    ins = V.bn_aggr(zmv[:, r % 2, q, :], zst[:, r % 2, q, :])
                ins.then_inc(sem("zvar"), 1)

            def last_norm(b, r):
                dve.wait_ge(sem("zrstd"), b * 6 + 6 * (r + 1))
                if not (isinstance(b, int) and b + r < 2):
                    dve.wait_ge(sem(f"stored{r % 2}"), b * 8 + 16 * (r // 2))
                for q in range(QB):
                    ins = V.tensor_scalar(o_t[:, r % 2, q, :], z_t[:, r % 2, q, :], zmv[:, r % 2, q, 0:1],
                                          zrs[:, r % 2, 3, q:q + 1], ALU.subtract, ALU.mult)
                ins.then_inc(sem("o_ready"), 1)

            for r in range(4):
                last_sum(0, r)
                if r:
                    last_norm(0, r - 1)
            with dve.Fori(4, NB - 3, 4) as b:
                for r in range(4):
                    last_sum(b, r)
                    last_norm(b, r - 1)
            last_norm(NB - 4, 3)


def kernel(**inputs):
    import numpy as np
    import concourse.bacc as bacc
    from concourse.bass_utils import run_bass_kernel_spmd

    names = ["L0_attn_x", "L0_attn_Wq", "L0_attn_Wk", "L0_attn_Wv", "L0_attn_Wo", "L0_attn_bo", "L0_ffn_gamma",
             "L0_ffn_beta", "L0_ffn_Wg", "L0_ffn_W1", "L0_ffn_b1", "L0_ffn_W2", "L0_ffn_b2"]
    nc = bacc.Bacc("TRN2", target_bir_lowering=False, num_devices=1)
    arrays = {n: np.ascontiguousarray(inputs[n]) for n in names}
    args = [nc.dram_tensor(n, arrays[n].shape, mybir.dt.from_np(arrays[n].dtype), kind="ExternalInput").ap()
            for n in names]
    out = nc.dram_tensor("out", arrays[names[0]].shape, F32, kind="ExternalOutput").ap()
    build_program(nc, *args, out)
    return run_bass_kernel_spmd(nc, [arrays], core_ids=[0]).results[0]["out"]
```

```python
from contextlib import ExitStack

import concourse.bass as bass
from concourse import mybir

F32 = mybir.dt.float32
F32R = mybir.dt.float32r
BF16 = mybir.dt.bfloat16
I32 = mybir.dt.int32
ALU = mybir.AluOpType
ACT = mybir.ActivationFunctionType
AX = mybir.AxisListType

P = 128
HD = 8
EPS = 1e-5
NEG = -1.0e30
SKIP = 1 << 24
ROW = 132


class At:

    def __init__(self, value, parity, loop):
        self.value, self.parity, self.loop = value, parity % 2, loop

    def plus(self, k):
        return At(self.value + k, self.parity + k, self.loop)

    def exists(self, n):
        return self.loop or 0 <= self.value < n


def wait_apart(eng, passed, sem, value):
    eng.wait_ge(sem, value)
    if not isinstance(value, int):
        eng.sem_inc(passed, 1)


def need(eng, sem, per, b, n, passed=None):
    if b.loop or b.value * per + n > 0:
        if passed is None:
            eng.wait_ge(sem, b.value * per + n)
        else:
            wait_apart(eng, passed, sem, b.value * per + n)


def build_program(nc, x, wq, wk, wv, wo, bo, gamma, beta, wg, w1, b1, w2, b2, out):
    NB, S, D = x.shape
    E, _, F = w1.shape
    NH = D // HD
    QB = S // P
    FC = F // P
    T = NB * S
    TOPK = 2
    REG = T + P
    NT = T * TOPK // P + E
    SCALE = float(HD) ** -0.5
    GH = 4
    UNITS = 3 * NH
    AUNITS = 3 * NH // 2
    ROUTE = 20
    RING = 8
    WEIGHTS = 6
    assert (S, D, NH, QB, FC, E) == (512, 128, 16, 4, 4, 8) and NB % 2 == 0 and NT % RING == 0

    x_rows = x.rearrange("b s d -> (b s) d")
    out_rows = out.rearrange("b s d -> (b s) d")
    rows_d = nc.dram_tensor("rows_d", (E * REG + E * P, ROW), F32, kind="Internal").ap()
    y_d = nc.dram_tensor("y_d", (T * TOPK, D), F32, kind="Internal").ap()
    qk_d = nc.dram_tensor("qk_d", (2, 2, 2, P, S), F32, kind="Internal").ap()
    att_d = nc.dram_tensor("att_d", (16, HD, NH, S // 16), F32, kind="Internal").ap()
    x2_d = nc.dram_tensor("x2_d", (T, D), F32, kind="Internal").ap()

    with ExitStack() as ctx:
        def sb(name, shape, dt=F32):
            return ctx.enter_context(nc.sbuf_tensor(name, shape, dt))

        def pb(name, shape):
            return ctx.enter_context(nc.psum_tensor(name, shape, F32))

        sems = {}

        def sem(name):
            if name not in sems:
                sems[name] = ctx.enter_context(nc.semaphore(name))
            return sems[name]

        kside = sb("kside", [P, 2, NH, S], F32R)
        qside = sb("qside", [P, 2, NH // GH, S], F32R)
        probs = sb("probs", [P, 8, 1280])
        vpad = sb("vpad", [P, 2, QB, NH, 32])
        xin = sb("xin", [P, 2, QB, D])
        xbo = sb("xbo", [P, 2, QB, D])
        xt = sb("xt", [P, S])
        qhl = sb("qhl", [P, 2, S], F32R)
        khl = sb("khl", [P, 2, S], F32R)
        ucp = sb("ucp", [P, S])
        urec = sb("urec", [P, QB, 8])
        att = sb("att", [P, QB, D])
        attt = sb("attt", [P, S])
        rows16 = sb("rows16", [P, S])
        ysum = sb("ysum", [P, QB, D])
        x1 = sb("x1", [P, QB, D])
        x2 = sb("x2", [P, QB, D])
        xc = sb("xc", [P, QB, D])
        xn = sb("xn", [P, 2, QB, TOPK, ROW])
        xnt = sb("xnt", [P, S])
        negmax = sb("negmax", [P, 2, QB, GH])
        mhl = sb("mhl", [P, QB, 2, GH], F32R)
        mt = sb("mt", [2 * GH, S])
        wq_s, wk_s, wv_s, wo_s = (sb(n, [P, D]) for n in ("wq_s", "wk_s", "wv_s", "wo_s"))
        wgt = sb("wgt", [P, E])
        bo_b, gam_b, bet_b = (sb(n, [P, D]) for n in ("bo_b", "gam_b", "bet_b"))
        ident = sb("ident", [P, P])
        identb = sb("identb", [P, P], BF16)
        maskb = sb("maskb", [P, P], BF16)
        lowerb = sb("lowerb", [P, P], BF16)
        onesb = sb("onesb", [P, P], BF16)
        stats = sb("stats", [P, 2, QB, 6])
        mv = sb("mv", [P, 2, QB, 2])
        rs = sb("rs", [P, 2, 6, QB])
        halfneg = sb("halfneg", [P, QB])
        lg = sb("lg", [P, QB, E])
        rt = sb("rt", [P, 12, QB, E])
        rv = sb("rv", [P, 8, QB])
        onehot = sb("onehot", [P, QB + 1, E], BF16)
        wtab = sb("wtab", [P, QB, E])
        wtab_i = sb("wtab_i", [P, QB, E], I32)
        used = sb("used", [P, E])
        first_row = sb("first_row", [P, E])
        tile_i = sb("tile_i", [P, NT], I32)
        tile_f = sb("tile_f", [P, NT])
        used_i = sb("used_i", [P, E], I32)
        slot = sb("slot", [P, 2, TOPK, QB], I32)
        gates = sb("gates", [P, NB * QB, TOPK])
        dest_i = sb("dest_i", [P, QB, TOPK], I32)
        dest = sb("dest", [P, QB, TOPK])
        w1_s = probs[:, :, :].rearrange("p r n -> p (r n)")[:, 0:E * F].rearrange("p (e f) -> p e f", e=E)
        w2_s = probs[:, :, :].rearrange("p r n -> p (r n)")[:, E * F:2 * E * F].rearrange(
            "p (e c d) -> p e c d", e=E, c=FC)
        w1_t = sb("w1_t", [P, 2, F])
        b1_s = sb("b1_s", [P, E, FC])
        b1_r = sb("b1_r", [E * FC, P])
        b2_b = vpad[:, 1].rearrange("p b h c -> p (b h c)")[:, 0:E * D].rearrange("p (e d) -> p e d", e=E)
        xs = sb("xs", [P, RING, ROW])
        xst = xnt[:].rearrange("p (r n) -> p r n", r=4)
        ht = vpad[:, 0].rearrange("p b h c -> p (b h c)").rearrange("p (r c n) -> p r c n", r=4, c=FC)
        ys = xbo[:].rearrange("p a q d -> p (a q) d")
        zrow = sb("zrow", [P, ROW])
        plan = sb("plan", [1, 3, NT])
        plan_i = sb("plan_i", [1, 2, NT], I32)
        cnt = sb("cnt", [1, 8, E])
        cnt_i = sb("cnt_i", [1, 3, E], I32)
        y_t = vpad[:, :, :, :, :].rearrange("p a b h c -> p (a b h c)").rearrange("p (r n) -> p r n", r=4)
        x2_t = probs[:, :, :].rearrange("p r n -> p (r n)")[:, 2 * E * F:2 * E * F + 4 * S].rearrange(
            "p (r n) -> p r n", r=4)
        flat = probs[:, :, :].rearrange("p r n -> p (r n)")
        z_t, o_t = (flat[:, 4 * S * k:4 * S * (k + 1)].rearrange("p (r q d) -> p r q d", r=4, q=QB) for k in range(2))
        zst = sb("zst", [P, 4, QB, 6])
        zmv = sb("zmv", [P, 4, QB, 2])
        zrs = sb("zrs", [P, 4, 6, QB])

        ps_s = pb("ps_s", [P, 2, 512])
        ps_a = pb("ps_a", [P, 4, 512])
        ps_v = pb("ps_v", [P, 512])
        ps_m = pb("ps_m", [P, 512])

        QSTART = [0, P, 2 * P, 3 * P]
        PCOL = {0: 0, 1: 512, 3: 896, 2: 1024}

        PER = {"xT": 1, "qT": 1, "kT": 1, "v": 1, "mT": 4, "uT": 2, "aT": 1, "wo": 1, "nT": 1}
        MISC = {0: ("xT", 1, 0), 1: ("mT", 0, 1), 2: ("kT", 1, 0), 3: ("qT", 1, 0), 4: ("v", 1, 0),
                5: ("mT", 0, 2), 6: ("uT", -1, 1), 7: ("aT", -1, 0), 9: ("mT", 0, 3), 10: ("nT", -2, 0),
                12: ("wo", -1, 0), 13: ("mT", 1, 0), 14: ("uT", 0, 0)}
        LG_STEP, RK_STEP = 12, 4
        in_spare = ps_a[:, 2, 3 * P:3 * P + (QB + 1) * E]
        IN_TURN = [MISC[h] for h in sorted(MISC)]

        MROW = 3 * GH * HD
        PLACED = (16 * 4, 16 * 12)

        def ready(stage):
            return sem("ready_" + stage)

        def freed(stage):
            return sem("freed_" + stage)

        def iterations(eng, body, first=-1):
            for i in range(first, 3):
                body(At(i, i, False))
            with eng.Fori(3, NB - 4, 2) as r:
                body(At(r, 1, True))
                body(At(r + 1, 0, True))
            for i in range(NB - 3, NB + 3):
                body(At(i, i, False))

        def tiles(eng, body):
            for t in range(RING):
                body(0, t)
            with eng.Fori(RING, NT - 2 * RING + 1, RING) as j:
                for t in range(RING):
                    body(j, t)
            for t in range(RING):
                body(NT - RING, t)

        def wait_from(eng, s, j, n):
            if isinstance(j, int) and j + n <= 0:
                return
            eng.wait_ge(s, j + n)

        def across(t, *shape):
            return t.unsqueeze(1).broadcast_to([P, *shape, t.shape[-1]])

        def along(t, n):
            return t.unsqueeze(len(t.shape)).broadcast_to([*t.shape, n])

        def place_max(act, b, g):
            if not b.exists(NB):
                return
            need(act, freed("mT"), 4, b, g + 1, sem("act_passed"))
            act.dma_start(qside[MROW:MROW + 2 * GH, b.parity, g, :].bitcast(F32), mt[:, :]).then_inc(
                sem("max_placed"), 16)

        def store_side(sp, b, side, what, hl):
            name = "qk"[what]
            if hl == 0:
                need(sp, sem(name + "_high"), 1, b, 1, sem("sp_passed"))
                need(sp, sem(name + "_placed"), PLACED[what], b, -PLACED[what], sem("sp_passed"))
            else:
                need(sp, freed(name + "T"), 1, b, 1, sem("sp_passed"))
            sp.dma_start(qk_d[b.parity, what, hl], side[:, hl, :].bitcast(F32)).then_inc(
                sem(f"{name}_stored{hl}"), 16)

        def place_side(sp, b, what, hl):
            name = "qk"[what]
            need(sp, sem(f"{name}_stored{hl}"), 16, b, 16, sem("sp_passed"))
            for part in range(3):
                if ((0, 0, 1), (0, 1, 0))[what][part] != hl:
                    continue
                r0 = GH * HD * part
                if what == 0:
                    of = qk_d[b.parity, 0, hl].rearrange("(g x) n -> x g n", x=GH * HD)
                    sp.dma_start(qside[r0:r0 + GH * HD, b.parity, :, :].bitcast(F32), of).then_inc(
                        sem("q_placed"), 16)
                    continue
                for hp in range(GH):
                    of = qk_d[b.parity, 1, hl].rearrange("(g h d) n -> h d g n", h=GH, d=HD)[hp]
                    r1 = r0 + HD * hp
                    sp.dma_start(kside[r1:r1 + HD, b.parity, hp:NH:GH, :].bitcast(F32), of).then_inc(
                        sem("k_placed"), 16)

        def body_sp(sp, i):
            nxt, prev, ahead = i.plus(1), i.plus(-1), i.plus(2)
            if ahead.exists(NB):
                need(sp, sem("xbo_ready"), 1, i, 1, sem("sp_passed"))
                need(sp, ready("xT"), 1, i, 1, sem("sp_passed"))
                sp.dma_start(xin[:, ahead.parity], x_rows[bass.ds(ahead.value * S, S), :].rearrange(
                    "(i p) d -> p i d", p=P)).then_inc(sem(f"x_in{ahead.parity}"), 16)
            if nxt.exists(NB):
                if not i.loop and i.value < 1:
                    sp.wait_ge(sem(f"kside_ones{nxt.parity}"), 16 * 2 * GH)
                    sp.wait_ge(sem("qside_zero"), nxt.parity + 1)
                need(sp, sem("scores_ready"), UNITS, i, 0, sem("sp_passed"))
                if i.exists(NB):
                    need(sp, sem("max_scores"), AUNITS, i, 1, sem("sp_passed"))
                z0 = MROW + 2 * GH
                sp.dma_start(qside[MROW:z0, nxt.parity, :, :].bitcast(F32),
                             kside[z0:z0 + 2 * GH, nxt.parity, 0:GH, :].bitcast(F32)).then_inc(sem("q_placed"), 16)
                store_side(sp, nxt, khl, 1, 0)
                store_side(sp, nxt, khl, 1, 1)
                place_side(sp, nxt, 1, 0)
                store_side(sp, nxt, qhl, 0, 0)
                store_side(sp, nxt, qhl, 0, 1)
                place_side(sp, nxt, 1, 1)
                place_side(sp, nxt, 0, 0)
                place_side(sp, nxt, 0, 1)
            if prev.plus(-1).exists(NB):
                b = prev.plus(-1)
                need(sp, sem("x2_ready"), 1, b, 1, sem("sp_passed"))
                sp.dma_start(x2_d[bass.ds(b.value * S, S), :].rearrange("(i p) d -> p i d", p=P),
                             x2[:, :, :]).then_inc(sem("x2_stored"), 16)
            if prev.exists(NB):
                need(sp, freed("aT"), 1, prev, 1, sem("sp_passed"))
                need(sp, sem("rows16_in"), 16, prev, 0, sem("sp_passed"))
                for d in range(HD):
                    sp.dma_start(att_d[:, d].rearrange("r h o -> h r o"),
                                 attt[d:P:HD, :].rearrange("h (r o) -> h r o", r=16)).then_inc(sem("att_stored"), 16)
                need(sp, sem("att_stored"), 16 * HD, prev, 16 * HD, sem("sp_passed"))
                need(sp, ready("wo"), 1, prev, 0, sem("sp_passed"))
                sp.dma_start(rows16[:, :], att_d.rearrange("r d h o -> (r d) (h o)")).then_inc(sem("rows16_in"), 16)

        block = ctx.enter_context(nc.Block())

        @block.sync
        def _(sp):
            sp.dma_start(xin[:, 0], x_rows[0:S, :].rearrange("(i p) d -> p i d", p=P)).then_inc(sem("x_in0"), 16)
            def load_heads(t, w, done):
                for k in range(2):
                    for p2 in range(2):
                        n = (8 * k + 4 * p2) * HD
                        of = w[:, 64 * k:64 * k + 64].rearrange("r (j p d) -> r p j d", j=GH, p=2)[:, p2]
                        sp.dma_start(t[:, n:n + GH * HD].rearrange("r (j d) -> r j d", j=GH), of).then_inc(
                            sem(done), 16)

            def place_ones(par):
                for hp in range(GH):
                    for half in range(2):
                        h0 = hp + 8 * half
                        sp.dma_start(kside[MROW + hp:MROW + 2 * GH:GH, par, h0:h0 + 5:GH, :].bitcast(F32),
                                     w1_t[0:2, :, :]).then_inc(sem(f"kside_ones{par}"), 16)

            load_heads(wk_s, wk, "head_weights")
            load_heads(wq_s, wq, "head_weights")
            load_heads(wv_s, wv, "head_weights")
            sp.wait_ge(sem("ones_ready"), 1)
            sp.wait_ge(sem("kside_zero0"), 2)
            place_ones(0)
            sp.dma_start(wo_s[:], wo).then_inc(sem("weights_in"), 16)
            body_sp(sp, At(-1, 1, False))
            for t, w in ((bo_b, bo), (gam_b, gamma), (bet_b, beta)):
                sp.dma_start(t[:], w.unsqueeze(0).broadcast_to([P, D])).then_inc(sem("weights_in"), 16)
            sp.dma_start(wgt[:, :], wg.rearrange("e d -> d e"),
                         allow_slow_non_contiguous=True).then_inc(sem("weights_in"), 16)
            sp.dma_start(b1_r[:, :], b1.rearrange("e (c p) -> (e c) p", p=P)).then_inc(sem("weights_in"), 16)
            sp.wait_ge(sem("kside_zero1"), 1)
            place_ones(1)
            sp.wait_ge(sem("zrow_ready"), 1)
            for e in range(E):
                sp.dma_start(rows_d[E * REG + e * P:E * REG + (e + 1) * P, :], zrow[:, :]).then_inc(
                    sem("pad_tiles"), 16)

            def body(i):
                if not i.loop and i.value == NB + 1:
                    sp.wait_ge(sem("pv_done"), 4 * NB)
                    sp.dma_start(w1_s, w1.rearrange("e p f -> p e f")).then_inc(sem("experts_in"), 16)
                    sp.dma_start(b2_b, b2.unsqueeze(0).broadcast_to([P, E, D])).then_inc(sem("experts_in"), 16)
                    for e in range(E):
                        sp.dma_start(w2_s[:, e], w2[e].rearrange("(c p) d -> p c d", p=P)).then_inc(
                            sem("experts_in"), 16)
                body_sp(sp, i)

            iterations(sp, body, first=0)
            sp.wait_ge(sem("ends_ready"), 1)
            for e in range(E):
                row = sp.value_load(cnt_i[0:1, 2, e:e + 1], min_val=0, max_val=E * REG - P)
                sp.dma_start(rows_d[bass.ds(row, P), :], zrow[:, :]).then_inc(sem("pad_tiles"), 16)
            sp.wait_ge(sem("plan_ready"), 1)
            sp.wait_ge(sem("rows_sent"), 16 * TOPK * QB * NB)
            sp.wait_ge(sem("pad_tiles"), 16 * 2 * E)

            def load_tile(j, t):
                row = sp.value_load(plan_i[0:1, 0, bass.ds(j + t, 1)], min_val=0, max_val=(E * REG + E * P - P))
                sp.dma_start(xs[:, t, :], rows_d[bass.ds(row, P), :]).then_inc(sem(f"tile_in{t}"), 16)

            for t in range(RING):
                load_tile(0, t)
            with sp.Fori(RING, NT - RING + 1, RING) as j:
                for t in range(RING):
                    wait_apart(sp, sem("sp_passed"), sem(f"sent{t}"), j * (16 // RING))
                    load_tile(j, t)
            for t in range(RING):
                sp.wait_ge(sem(f"sent{t}"), 16 * (NT // RING))
            sp.wait_ge(sem("x2_stored"), 16 * NB)

            def load_last(b, r):
                sp.dma_start(y_t[:, r].rearrange("p (i n) -> p i n", i=QB),
                             y_d[bass.ds(b * (S * TOPK), S * TOPK), :].rearrange(
                                 "(i p k) d -> p i (k d)", p=P, k=TOPK)).then_inc(sem(f"y_in{r}"), 16)
                sp.dma_start(x2_t[:, r].rearrange("p (i n) -> p i n", i=QB),
                             x2_d[bass.ds(b * S, S), :].rearrange("(i p) d -> p i d", p=P)).then_inc(
                                 sem(f"y_in{r}"), 16)

            def store_last(b, r):
                wait_apart(sp, sem("sp_passed"), sem("o_ready"), b + 1)
                sp.dma_start(out_rows[bass.ds(b * S, S), :].rearrange("(i p) d -> p i d", p=P),
                             o_t[:, r]).then_inc(sem(f"stored{r}"), 16)

            for r in range(4):
                load_last(r, r)
            with sp.Fori(0, NB - 7, 4) as b:
                for r in range(4):
                    wait_apart(sp, sem("sp_passed"), sem("z_done"), b + (r + 1))
                    load_last(b + (r + 4), r)
                    store_last(b + r, r)
            for r in range(4):
                store_last(NB - 4 + r, r)
            for r in range(4):
                sp.wait_ge(sem(f"stored{r}"), 16 * (NB // 4))

        @block.gpsimd
        def _(pool):
            chain = [0]

            def link(ins):
                chain[0] += 1
                ins.then_inc(sem("pool_chain"), 1)
                pool.wait_ge(sem("pool_chain"), chain[0])

            pool.memset(ident[:], 0.0)
            pool.memset(identb[:], 0.0)
            pool.memset(onesb[:], 1.0)
            pool.memset(maskb[:], 0.0)
            pool.memset(halfneg[:], -0.5)
            link(pool.memset(lowerb[:], 0.0))
            for m in (ident, identb):
                pool.affine_select(out=m[:], in_=m[:], pattern=[[-1, P]], compare_op=ALU.not_equal, fill=1.0,
                                   base=0, channel_multiplier=1)
            pool.affine_select(out=maskb[:], in_=maskb[:], pattern=[[-1, P]], compare_op=ALU.is_ge, fill=NEG,
                               base=0, channel_multiplier=1)
            pool.affine_select(out=lowerb[:], in_=lowerb[:], pattern=[[-1, P]], compare_op=ALU.is_ge,
                               fill=1.0, base=0, channel_multiplier=1).then_inc(sem("consts"), 1)
            pool.memset(kside[:, 0, NH // 2:NH].bitcast(F32), 0.0).then_inc(sem("kside_zero0"), 1)
            pool.memset(qside[:, 0].bitcast(F32), 0.0).then_inc(sem("qside_zero"), 1)
            pool.memset(vpad[:, 0], 0.0)
            link(pool.memset(vpad[:, 1], 0.0))
            vh = vpad[:, :, :, :, :].rearrange("p a b (k g j) c -> p (a b k) g j c", k=2, g=2)
            pool.memset(vh[:, :, 0, :, 8:16], 1.0)
            pool.memset(vh[:, :, 1, :, 24:32], 1.0).then_inc(sem("vpad_set"), 1)
            pool.iota(wtab_i[:], pattern=[[0, QB], [-1, E]], base=E, channel_multiplier=0)
            pool.iota(used_i[:], pattern=[[REG, E]], base=0, channel_multiplier=0)
            pool.iota(dest_i[:], pattern=[[TOPK * P, QB], [1, TOPK]], base=0, channel_multiplier=TOPK)
            pool.iota(tile_i[:], pattern=[[1, NT]], base=0, channel_multiplier=0)
            pool.memset(xn[:], 0.0)
            link(pool.memset(zrow[:], 0.0))
            pool.tensor_copy(wtab[:], wtab_i[:])
            pool.tensor_copy(used[:], used_i[:])
            pool.tensor_copy(first_row[:], used_i[:])
            pool.tensor_copy(tile_f[:], tile_i[:])
            pool.tensor_copy(dest[:], dest_i[:])
            link(pool.memset(zrow[:, D:D + 1].bitcast(I32), SKIP))
            pool.memset(onehot[:], 0.0).then_inc(sem("zrow_ready"), 1)
            pool.memset(qside[:, 1].bitcast(F32), 0.0).then_inc(sem("qside_zero"), 1)
            pool.memset(kside[:, 1].bitcast(F32), 0.0).then_inc(sem("kside_zero1"), 1)

            def body(i):
                nxt, prev, rb, late = i.plus(1), i.plus(-1), i.plus(-2), i.plus(-3)
                for h in range(NH):
                    if i.exists(NB):
                        need(pool, sem("exp_done"), UNITS, i, 3 * h + 2, sem("pool_passed"))
                        pr = probs[:, h % 8, :]
                        first = pr[:, 0:1024].rearrange("p (a n) -> p a n", a=2)[:, :, 0:P]
                        pool.affine_select(out=first, in_=first, pattern=[[0, 2], [1, P]],
                                           compare_op=ALU.is_ge, fill=0.0, base=0,
                                           channel_multiplier=-1).then_inc(sem("masked"), 1)
                        need(pool, sem("exp_done"), UNITS, i, 3 * h + 3, sem("pool_passed"))
                        last = pr[:, 896:1152].rearrange("p (a n) -> p a n", a=2)
                        pool.affine_select(out=last, in_=last, pattern=[[0, 2], [1, P]],
                                           compare_op=ALU.is_ge, fill=0.0, base=0,
                                           channel_multiplier=-1).then_inc(sem("masked"), 1)
                    if rb.exists(NB) and 7 <= h <= 9:
                        make_rows(pool, rb, h - 7)
                    if late.exists(NB) and 6 <= h <= 13:
                        q, k = (h - 6) // 2, (h - 6) % 2
                        if h == 6:
                            need(pool, sem("rows_sent"), 16 * TOPK * QB, late, 0, sem("pool_passed"))
                            need(pool, sem("slot_ready"), 1, late, 1, sem("pool_passed"))
                            need(pool, sem("xn_ready"), 1, late, 1, sem("pool_passed"))
                        pool.indirect_dma_start(
                            rows_d, bass.IndirectOffsetOnAxis(ap=slot[:, late.parity, k, q:q + 1], axis=0),
                            xn[:, late.parity, q, k, :], None).then_inc(sem("rows_sent"), 16)
                    if nxt.exists(NB) and h == 15:
                        need(pool, freed("wo"), 1, prev, 1, sem("pool_passed"))
                        need(pool, sem(f"x_in{nxt.parity}"), 8, nxt, 16 - 8 * nxt.parity, sem("pool_passed"))
                        if not i.loop and i.value < 0:
                            pool.wait_ge(sem("weights_in"), 16 * WEIGHTS)
                        pool.tensor_tensor(xbo[:, nxt.parity], xin[:, nxt.parity], across(bo_b[:], QB),
                                           ALU.add).then_inc(sem("xbo_ready"), 1)
                    if prev.exists(NB) and h == 14:
                        need(pool, sem("x1_ready"), 1, prev, 0, sem("pool_passed"))
                        rstd(pool, prev, 0)
                    if rb.exists(NB):
                        if h == 3:
                            need(pool, sem("xc_ready"), 1, rb, 0, sem("pool_passed"))
                            rstd(pool, rb, 1)
                        if h == 4:
                            need(pool, sem("x2_stored"), 16, rb, 0, sem("pool_passed"))
                            pool.tensor_scalar(x2[:], x1[:], 2.0, None, ALU.mult).then_inc(sem("x2_ready"), 1)

            def rstd(pool, b, which):
                need(pool, sem(f"var{which}"), 1, b, 1, sem("pool_passed"))
                v, r, s, t, n, m = (rs[:, which, k, :] for k in range(6))
                pool.tensor_scalar(n, mv[:, which, :, 0], -1.0, None, ALU.mult)
                for k, step in enumerate((
                        lambda: pool.tensor_scalar(v, mv[:, which, :, 1], EPS, None, ALU.add),
                        lambda: pool.tensor_tensor(r, v, halfneg[:], ALU.pow),
                        lambda: pool.tensor_tensor(s, r, r, ALU.mult),
                        lambda: pool.tensor_tensor(s, s, v, ALU.mult),
                        lambda: pool.tensor_scalar(s, s, -0.5, 1.5, ALU.mult, ALU.add),
                        lambda: pool.tensor_tensor(t, r, s, ALU.mult),
                        lambda: pool.tensor_tensor(m, n, t, ALU.mult))):
                    if k:
                        need(pool, sem(f"rstd{which}"), 7, b, k, sem("pool_passed"))
                    step().then_inc(sem(f"rstd{which}"), 1)

            def make_rows(pool, b, part):
                if part == 0:
                    need(pool, sem("xc_ready"), 1, b, 1, sem("pool_passed"))
                    pool.tensor_tensor(xc[:], xc[:], across(gam_b[:], QB), ALU.mult).then_inc(sem("xn_steps"), 1)
                if part == 1:
                    need(pool, ready("nT"), 1, b.plus(-1), 0, sem("pool_passed"))
                    pool.tensor_copy(xn[:, b.parity, :, :, D].bitcast(I32), dest[:]).then_inc(sem("xn_steps"), 1)
                    need(pool, sem("xn_steps"), 4, b, 2, sem("pool_passed"))
                    pool.tensor_tensor(xn[:, b.parity, :, 0, 0:D], xc[:], across(bet_b[:], QB),
                                       ALU.add).then_inc(sem("xn_steps"), 1)
                    pool.tensor_scalar(dest[:], dest[:], float(TOPK * S), None, ALU.add).then_inc(sem("xn_steps"), 1)
                if part == 2:
                    need(pool, sem("xn_steps"), 4, b, 4, sem("pool_passed"))
                    pool.tensor_copy(xn[:, b.parity, :, 1, 0:D], xn[:, b.parity, :, 0, 0:D]).then_inc(
                        sem("xn_ready"), 1)

            iterations(pool, body)

            def send(j, t):
                wait_apart(pool, sem("pool_passed"), sem("ys_ready"), j + (t + 1))
                pool.indirect_dma_start(
                    y_d, bass.IndirectOffsetOnAxis(ap=xs[:, t, D:D + 1].bitcast(I32), axis=0), ys[:, t, :], None,
                    bounds_check=T * TOPK - 1, oob_is_err=False).then_inc(sem(f"sent{t}"), 16)

            tiles(pool, send)

            def zrstd(b, r):
                wait_apart(pool, sem("pool_passed"), sem("zvar"), b + (r + 1))
                v, s, u, t, n, m = (zrs[:, r, k, :] for k in range(6))
                pool.tensor_scalar(n, zmv[:, r, :, 0], -1.0, None, ALU.mult)
                for k, step in enumerate((
                        lambda: pool.tensor_scalar(v, zmv[:, r, :, 1], EPS, None, ALU.add),
                        lambda: pool.tensor_tensor(s, v, halfneg[:], ALU.pow),
                        lambda: pool.tensor_tensor(u, s, s, ALU.mult),
                        lambda: pool.tensor_tensor(u, u, v, ALU.mult),
                        lambda: pool.tensor_scalar(u, u, -0.5, 1.5, ALU.mult, ALU.add),
                        lambda: pool.tensor_tensor(t, s, u, ALU.mult),
                        lambda: pool.tensor_tensor(m, n, t, ALU.mult))):
                    if k:
                        wait_apart(pool, sem("pool_passed"), sem("zrstd"), b * 7 + (7 * r + k))
                    step().then_inc(sem("zrstd"), 1)

            with pool.Fori(0, NB - 3, 4) as b:
                for r in range(4):
                    zrstd(b, r)

        @block.scalar
        def _(act):
            def body(i):
                nxt, prev, rb = i.plus(1), i.plus(-1), i.plus(-2)
                for h in range(NH):
                    if h == 4 and prev.exists(NB):
                        copy_u(act, prev, 1)
                    if h == 12 and i.exists(NB):
                        copy_u(act, i, 0)
                    for u in range(3):
                        if i.exists(NB):
                            if h % 4 == 0 and u == 0:
                                need(act, sem("pv_done"), 4, i, h // 4 - 1)
                            n = 3 * h + u
                            need(act, sem("scores_ready"), UNITS, i, n + 1)
                            c0, to = ((0, 0), (P, 512), (P, 896))[u]
                            nc.scalar.activation(probs[:, h % 8, to:to + 512 - c0], ps_s[:, n % 2, c0:512],
                                                 ACT.Exp, scale=SCALE).then_inc(sem("exp_done"), 1)
                        if u != 1 and h in (0, 1) and rb.exists(NB):
                            if h == 0 and u == 0:
                                need(act, sem("x2_ready"), 1, rb, 0)
                            normalize(rb, 0, 2 * h + u // 2, x1, ysum, "x1_ready")
                        if u != 1 and h in (5, 6) and rb.exists(NB):
                            if h == 5 and u == 0:
                                need(act, sem("xn_ready"), 1, rb, 0)
                            normalize(rb, 1, 2 * (h - 5) + u // 2, xc, x1, "xc_ready")
                        if u == 1:
                            middle(act, h, i, nxt, prev, rb)
                            if h % 4 == 2:
                                place_max(act, *((i, 1), (i, 2), (i, 3), (nxt, 0))[h // 4])

            def copy_v(act, b):
                need(act, ready("v"), 1, b, 1)
                need(act, sem("pv_done"), 4, b.plus(-1), 0)
                if not b.loop and b.value == 0:
                    act.wait_ge(sem("vpad_set"), 1)
                of = ps_m[:].rearrange("p (a g j d) -> p a g j d", a=2 * QB, g=2, j=GH)
                to = vpad[:, b.parity].rearrange("p b (k g j) c -> p (b k) g j c", k=2, g=2)
                nc.scalar.activation(to[:, :, 0, :, 0:HD], of[:, :, 0], ACT.Copy)
                nc.scalar.activation(to[:, :, 1, :, 16:16 + HD], of[:, :, 1], ACT.Copy).then_inc(freed("v"), 1)

            def normalize(b, which, q, dst, src, done):
                if q == 0:
                    need(act, sem(f"rstd{which}"), 7, b, 7)
                ins = nc.scalar.activation(dst[:, q, :], src[:, q, :], ACT.Identity,
                                           bias=rs[:, which, 5, q:q + 1], scale=rs[:, which, 3, q:q + 1])
                if q == QB - 1:
                    ins.then_inc(sem(done), 1)

            def copy_u(act, b, k):
                need(act, sem("pv_done"), 4, b, 2 * k + 2)
                need(act, ready("uT"), 2, b, k)
                nc.scalar.activation(ucp[:], ps_v[:], ACT.Copy).then_inc(sem("u_copied"), 1)

            def middle(act, h, i, nxt, prev, rb):
                if nxt.exists(NB):
                    if h == 0:
                        need(act, ready("xT"), 1, nxt, 1)
                        need(act, ready("v"), 1, nxt, 0)
                        nc.scalar.activation(xt[:], ps_m[:], ACT.Copy).then_inc(freed("xT"), 1)
                    if h == 4:
                        copy_v(act, nxt)
                    if h == 3:
                        need(act, ready("qT"), 1, nxt, 1)
                        need(act, sem("q_stored0"), 16, nxt, 0)
                        need(act, sem("q_stored1"), 16, nxt, 0)
                        nc.scalar.activation(qhl[:, 0], ps_m[:], ACT.Copy).then_inc(sem("q_high"), 1)
                    if h == 2:
                        need(act, ready("kT"), 1, nxt, 1)
                        need(act, sem("k_stored0"), 16, nxt, 0)
                        need(act, sem("k_stored1"), 16, nxt, 0)
                        nc.scalar.activation(khl[:, 0], ps_m[:], ACT.Copy).then_inc(sem("k_high"), 1)
                if rb.exists(NB):
                    if h == 10:
                        need(act, ready("nT"), 1, rb, 1)
                        need(act, ready("lg"), 1, rb, 0)
                        nc.scalar.activation(xnt[:], ps_m[:], ACT.Copy).then_inc(freed("nT"), 1)
                    if h == 15:
                        need(act, sem("route"), ROUTE, rb, 2)
                        nc.scalar.activation(rt[:, 2], rt[:, 1], ACT.Exp).then_inc(sem("gate_exp"), 1)
                if h == 3 and i.plus(-3).exists(NB):
                    need(act, sem("route"), ROUTE, i.plus(-3), 8)
                    nc.scalar.activation(rv[:, 4], rv[:, 3], ACT.Exp).then_inc(sem("gate_exp"), 1)
                if prev.exists(NB):
                    if h == 7:
                        need(act, ready("aT"), 1, prev, 1)
                        need(act, sem("att_stored"), 16 * HD, prev, 0)
                        nc.scalar.activation(attt[:].rearrange("p (r o) -> p o r", r=16),
                                             ps_m[:].rearrange("p (o r) -> p o r", r=16),
                                             ACT.Copy).then_inc(freed("aT"), 1)

            iterations(act, body)

            act.wait_ge(sem("plan_ready"), 1)
            act.wait_ge(sem("b1_ready"), 1)

            def hidden(j, t):
                e = act.value_load(plan_i[0:1, 1, bass.ds(j + t, 1)], min_val=0, max_val=E - 1)
                act.wait_ge(sem("h_ready"), j + (t + 1))
                wait_from(act, sem("y_ready"), j, t - 3)
                for c in range(FC):
                    ins = nc.scalar.activation(ht[:, t % 4, c, :], ps_a[:, t % 4, c * P:(c + 1) * P],
                                               ACT.Gelu_apprx_tanh,
                                               bias=b1_s[:, bass.ds(e, 1), c:c + 1].rearrange("p a b -> p (a b)"))
                ins.then_inc(sem("ht_ready"), 1)

            tiles(act, hidden)

            def last_norm(b, r):
                act.wait_ge(sem("zrstd"), b * 7 + 7 * (r + 1))
                if not isinstance(b, int):
                    act.wait_ge(sem(f"stored{r}"), b * 4)
                for q in range(QB):
                    ins = nc.scalar.activation(o_t[:, r, q, :], z_t[:, r, q, :], ACT.Identity,
                                               bias=zrs[:, r, 5, q:q + 1], scale=zrs[:, r, 3, q:q + 1])
                ins.then_inc(sem("o_ready"), 1)

            for r in range(4):
                last_norm(0, r)
            with act.Fori(4, NB - 3, 4) as b:
                for r in range(4):
                    last_norm(b, r)

        @block.tensor
        def _(pe):
            turn = {}

            def misc(i, name, off, place):
                b = i.plus(off)
                if not b.exists(NB):
                    return
                at = IN_TURN.index((name, off, place))
                for back in range(1, len(IN_TURN)):
                    n2, off2, place2 = IN_TURN[(at - back) % len(IN_TURN)]
                    b2_ = i.plus(off2 - (1 if at - back < 0 else 0))
                    if b2_.exists(NB):
                        need(pe, freed(n2), PER[n2], b2_, place2 + 1)
                        break
                stages[name](b, place).then_inc(ready(name), 1)

            def tr(src):
                for q in range(QB):
                    ins = pe.transpose(ps_m[:, q * P:(q + 1) * P], src(q), ident[:])
                return ins

            def st_xT(b, place):
                need(pe, sem(f"x_in{b.parity}"), 8, b, 16 - 8 * b.parity)
                return tr(lambda q: xin[:, b.parity, q, :])

            def st_kT(b, place):
                need(pe, freed("xT"), 1, b, 1)
                if not b.loop and b.value == 0:
                    pe.wait_ge(sem("head_weights"), 16 * 12)
                return pe.matmul(ps_m[:], wk_s[:], xt[:], start=True, stop=True)

            def st_qT(b, place):
                return pe.matmul(ps_m[:], wq_s[:], xt[:], start=True, stop=True)

            def st_v(b, place):
                for q in range(QB):
                    ins = pe.matmul(ps_m[:, q * P:(q + 1) * P], xt[:, q * P:(q + 1) * P], wv_s[:],
                                    start=True, stop=True)
                return ins

            def st_mT(b, g):
                need(pe, sem("max_split"), 8, b, 2 * g + 2)
                for q in range(QB):
                    ins = pe.transpose(ps_m[0:2 * GH, q * P:(q + 1) * P],
                                       mhl[:, q].bitcast(F32).rearrange("p a b -> p (a b)"), ident[:])
                return ins

            def st_uT(b, k):
                need(pe, sem("u_copied"), 2, b, k + 1)
                return tr(lambda q: ucp[:, q * P:(q + 1) * P])

            def st_aT(b, place):
                need(pe, freed("uT"), 2, b, 2)
                return tr(lambda q: att[:, q, :])

            def st_wo(b, place):
                need(pe, sem("rows16_in"), 16, b, 16)
                if not b.loop and b.value == 0:
                    pe.wait_ge(sem("weights_in"), 16 * WEIGHTS)
                for q in range(QB):
                    ins = pe.matmul(ps_m[:, q * P:(q + 1) * P], rows16[:, q * P:(q + 1) * P], wo_s[:],
                                    start=True, stop=True)
                return ins

            def st_nT(b, place):
                need(pe, sem("xn_steps"), 4, b, 4)
                return tr(lambda q: xn[:, b.parity, q, 0, 0:D])

            def spare(i, mb, h):
                b = i.plus(-2 if h == LG_STEP else -3)
                if h not in (LG_STEP, RK_STEP) or not b.exists(NB):
                    return
                if not mb.exists(NB):
                    pe.wait_ge(sem("max_taken"), AUNITS * NB)
                if h == LG_STEP:
                    need(pe, freed("nT"), 1, b, 1)
                    need(pe, sem("route"), ROUTE, b.plus(-1), 14)
                    for q in range(QB):
                        ins = pe.matmul(in_spare[:, q * E:(q + 1) * E], xnt[:, q * P:(q + 1) * P],
                                        wgt[:], start=True, stop=True)
                    ins.then_inc(ready("lg"), 1)
                    return
                need(pe, sem("route"), ROUTE, b, 12)
                pe.matmul(in_spare, lowerb[:], onehot[:].rearrange("p a e -> p (a e)"), start=True,
                          stop=False)
                for s in range(QB):
                    ins = pe.matmul(in_spare[:, (s + 1) * E:].rearrange("p (a e) -> p a e", e=E), onesb[:],
                                    across(onehot[:, s, :], QB - s), start=False, stop=(s == QB - 1))
                ins.then_inc(ready("rk"), 1)

            stages = dict(xT=st_xT, qT=st_qT, kT=st_kT, v=st_v, mT=st_mT, uT=st_uT, aT=st_aT, wo=st_wo,
                          nT=st_nT)

            def scores(i, h, u):
                if not i.exists(NB):
                    return
                g, n = h // GH, 3 * h + u
                if h % GH == 0 and u == 0:
                    need(pe, sem("max_placed"), 16 * 4, i, 16 * (g + 1))
                need(pe, sem("exp_done"), UNITS, i, n - 1)
                for kb, q0, c0 in (((0, 0, 0),), ((1, P, P),), ((3, 2 * P, 0), (2, 2 * P, 2 * P)))[u]:
                    ins = pe.matmul(ps_s[:, n % 2, c0:c0 + S - q0], kside[:, i.parity, h, kb * P:(kb + 1) * P],
                                    qside[:, i.parity, g, q0:S], start=True, stop=True)
                ins.then_inc(sem("scores_ready"), 1)

            def maxima(b, n, i, h):
                if not b.exists(NB):
                    if n % 3 == 1:
                        spare(i, b, h)
                    return
                if n == 0:
                    need(pe, sem("q_placed"), PLACED[0], b, PLACED[0])
                    need(pe, sem("k_placed"), PLACED[1], b, PLACED[1])
                need(pe, sem("max_taken"), AUNITS, b, n - 1)
                if n % 3 == 1:
                    spare(i, b, h)
                for s in range(2):
                    h = 2 * (n // 3) + s
                    to = ps_a[:, 2 * (n % 2) + s, :]
                    blocks = (((3, S, 0),), ((2, 3 * P, 0),), ((0, 2 * P, 0), (1, 2 * P, 2 * P)))[n % 3]
                    for qb, nk, c0 in blocks:
                        pe.matmul(to[:, c0:c0 + nk], qside[:, b.parity, h // GH, qb * P:(qb + 1) * P],
                                  kside[:, b.parity, h, 0:nk], start=(c0 == 0), stop=False)
                    if n % 3 == 2:
                        ins = pe.matmul(to.rearrange("p (a n) -> p a n", n=P)[:, 0:QB:QB - 1, :], identb[:],
                                        across(maskb[:], 2), start=False, stop=True)
                    else:
                        c1 = qb * P
                        ins = pe.matmul(to[:, c1:c1 + P], identb[:], maskb[:], start=False, stop=True)
                ins.then_inc(sem("max_scores"), 1)

            def values(b, g, kbs):
                if not b.exists(NB):
                    return
                if kbs[0] == 0:
                    need(pe, sem("masked"), 2 * NH, b, 2 * GH * (g + 1))
                    if g == 0:
                        need(pe, freed("v"), 1, b, 1)
                    if g % 2 == 0:
                        need(pe, sem("u_copied"), 2, b, g // 2)
                for kb in kbs:
                    for j in range(GH):
                        h = GH * g + j
                        c = PCOL[kb]
                        ins = pe.matmul(ps_v[32 * j:32 * j + 32, kb * P:S], vpad[:, b.parity, kb, h, :],
                                        probs[:, h % 8, c:c + S - kb * P],
                                        start=(g % 2 == 0 and kb == 0), stop=(g % 2 == 1 and kb == kbs[-1] == 2),
                                        skip_group_check=True)
                if kbs[-1] == 2:
                    ins.then_inc(sem("pv_done"), 1)

            pe.wait_ge(sem("consts"), 1)

            def body(i):
                for h in range(NH):
                    mb, mg = (i, h // 4 + 2) if h < 8 else (i.plus(1), h // 4 - 2)
                    mu = 6 * mg + 3 * (h % 4 // 2)
                    scores(i, h, 0)
                    maxima(mb, mu + (2 if h % 2 else 0), i, h)
                    scores(i, h, 1)
                    if h in MISC:
                        misc(i, *MISC[h])
                    if h % 2 == 0:
                        maxima(mb, mu + 1, i, h)
                    scores(i, h, 2)
                    if h % 4:
                        vb, vg = (i, h // 4 - 1) if h >= 4 else (i.plus(-1), 3)
                        values(vb, vg, ((0,), (1,), (3, 2))[h % 4 - 1])

            iterations(pe, body)

            pe.wait_ge(sem("weights_in"), 16 * WEIGHTS)
            pe.wait_ge(sem("route"), ROUTE * NB)
            pe.transpose(ps_m[:, 0:E * FC], b1_r[:, :], ident[0:E * FC, 0:E * FC]).then_inc(sem("b1_turned"), 1)
            pe.wait_ge(sem("b1_ready"), 1)
            pe.wait_ge(sem("plan_ready"), 1)
            pe.wait_ge(sem("experts_in"), 16 * (E + 2))

            def turn_tile(j, t):
                pe.wait_ge(sem(f"tile_in{t % RING}"), j * (16 // RING) + 16 * (t // RING + 1))
                wait_from(pe, sem("xst_ready"), j, t - 1)
                to = (ps_m, ps_v)[t % 2]
                pe.transpose(to[:, 0:P], xs[:, t % RING, 0:D], ident[:]).then_inc(sem("tile_turned"), 1)

            def first_product(j, t):
                pe.wait_ge(sem("xst_ready"), j + (t + 1))
                pe.wait_ge(sem("w1_ready"), j + (t + 1))
                wait_from(pe, sem("ht_ready"), j, t - 3)
                for c in range(FC):
                    ins = pe.matmul(ps_a[:, t % 4, c * P:(c + 1) * P], w1_t[:, t % 2, c * P:(c + 1) * P],
                                    xst[:, t % 4, :], start=True, stop=True)
                ins.then_inc(sem("h_ready"), 1)

            def second_product(j, t):
                e = pe.value_load(plan_i[0:1, 1, bass.ds(j + t, 1)], min_val=0, max_val=E - 1)
                pe.wait_ge(sem("ht_ready"), j + (t + 1))
                wait_from(pe, sem("ys_ready"), j, t - 1)
                for c in range(FC):
                    ins = pe.matmul(ps_s[:, t % 2, 0:D], ht[:, t % 4, c, :],
                                    w2_s[:, bass.ds(e, 1), c, :].rearrange("p a d -> p (a d)"),
                                    start=(c == 0), stop=(c == FC - 1))
                ins.then_inc(sem("y_ready"), 1)

            def tile(j, t):
                last = isinstance(j, int) and j + t == NT - 1
                first_product(j, t)
                if not (isinstance(j, int) and j + t >= NT - 2):
                    turn_tile(j, t + 2)
                if not (isinstance(j, int) and j + t == 0):
                    second_product(j, t - 1)
                if last:
                    second_product(j, t)

            turn_tile(0, 0)
            turn_tile(0, 1)
            tiles(pe, tile)

        @block.vector
        def _(dve):
            dve.memset(w1_t[0:2, :, :], 1.0).then_inc(sem("ones_ready"), 1)
            dve.memset(kside[:, 0, 0:NH // 2].bitcast(F32), 0.0).then_inc(sem("kside_zero0"), 1)

            def maximum(b, n, part):
                if not b.exists(NB):
                    return
                need(dve, sem("max_scores"), AUNITS, b, n + 1)
                qb, nk, c0 = (((3, S, 0),), ((2, 3 * P, 0),), ((1, 2 * P, 2 * P), (0, P, 0)))[n % 3][part]
                s = 2 * (n // 3 % 2)
                ins = nc.vector.tensor_reduce(
                    negmax[:, n // 6 % 2, qb, s:s + 2], ps_a[:, 2 * (n % 2):2 * (n % 2) + 2, c0:c0 + nk], AX.X, ALU.max,
                    negate=True)
                if n % 3 < 2 or part == 1:
                    ins.then_inc(sem("max_taken"), 1)

            def split_max(b, g, low):
                if not b.exists(NB):
                    return
                if not low:
                    need(dve, sem("max_taken"), AUNITS, b, 6 * (g + 1))
                    need(dve, ready("mT"), 4, b, g)
                    nc.vector.tensor_copy(mhl[:, :, 0, :], negmax[:, g % 2]).then_inc(sem("max_split"), 1)
                else:
                    need(dve, sem("max_split"), 8, b, 2 * g + 1)
                    nc.vector.tensor_tensor(mhl[:, :, 1, :], negmax[:, g % 2], mhl[:, :, 0, :].bitcast(F32),
                                            ALU.subtract).then_inc(sem("max_split"), 1)

            def copy_max(b, g):
                if not b.exists(NB):
                    return
                need(dve, ready("mT"), 4, b, g + 1)
                need(dve, sem("max_placed"), 64, b, 16 * g)
                nc.vector.tensor_copy(mt[:], ps_m[0:2 * GH, :]).then_inc(freed("mT"), 1)

            def low_part(b, side, name, high, stage):
                need(dve, sem(high), 1, b, 1)
                nc.vector.tensor_tensor(side[:, 1], ps_m[:], side[:, 0].bitcast(F32),
                                        ALU.subtract).then_inc(freed(stage), 1)

            def divide(b, k, second):
                of = ps_m[:].rearrange("p (q a c) -> p q a c", q=QB, c=16)
                if not second:
                    need(dve, ready("uT"), 2, b, k + 1)
                    nc.vector.reciprocal(urec[:], of[:, :, :, 8]).then_inc(sem("recip"), 1)
                else:
                    need(dve, sem("recip"), 2, b, k + 1)
                    need(dve, ready("aT"), 1, b, 0)
                    nc.vector.tensor_tensor(att[:, :, 64 * k:64 * k + 64].rearrange("p q (a d) -> p q a d", d=HD),
                                            of[:, :, :, 0:HD], along(urec[:], HD), ALU.mult).then_inc(freed("uT"), 1)

            def statistics(b, which, src):
                for q in range(QB):
                    ins = nc.vector.bn_stats(stats[:, which, q, :], src[:, q, :])
                ins.then_inc(sem("stats"), 1)

            def aggregate(b, which):
                need(dve, sem("stats"), 2, b, which + 1, sem("dve_passed"))
                for q in range(QB):
                    ins = nc.vector.bn_aggr(mv[:, which, q, :], stats[:, which, q, :])
                ins.then_inc(sem(f"var{which}"), 1)

            V = nc.vector
            best, d_best, z, e2, c1, v2, c2 = (rv[:, k] for k in (0, 3, 6, 4, 1, 2, 5))
            eq1, diff, ex, w1c, m1, rest, eq2, w2c, m2, place, p1, p2 = (rt[:, k] for k in range(12))

            def g(b, k):
                return gates[:, bass.ds(b.value * QB, QB), k]

            ROUTING = [
                lambda b: [V.tensor_reduce(best, lg[:], AX.X, ALU.max)],
                lambda b: [V.tensor_tensor(eq1, lg[:], along(best, E), ALU.is_equal),
                           V.tensor_tensor(diff, lg[:], along(best, E), ALU.subtract)],
                lambda b: [V.tensor_tensor(w1c, eq1, wtab[:], ALU.mult)],
                lambda b: [V.tensor_reduce(c1, w1c, AX.X, ALU.max)],
                lambda b: [V.tensor_tensor(m1, wtab[:], along(c1, E), ALU.is_equal)],
                lambda b: [V.scalar_tensor_tensor(out=rest, in0=m1, scalar=NEG, in1=lg[:], op0=ALU.mult,
                                                  op1=ALU.add)],
                lambda b: [V.tensor_reduce(v2, rest, AX.X, ALU.max)],
                lambda b: [V.tensor_tensor(eq2, rest, along(v2, E), ALU.is_equal),
                           V.tensor_tensor(d_best, v2, best, ALU.subtract)],
                lambda b: [V.tensor_tensor(w2c, eq2, wtab[:], ALU.mult)],
                lambda b: [V.tensor_reduce(c2, w2c, AX.X, ALU.max)],
                lambda b: [V.tensor_tensor(m2, wtab[:], along(c2, E), ALU.is_equal)],
                lambda b: [V.tensor_tensor(onehot[:, 0:QB, :], m1, m2, ALU.add)],
                lambda b: [V.tensor_tensor(place, in_spare[:, 0:QB * E].rearrange("p (q e) -> p q e", e=E),
                                           across(used[:], QB), ALU.add)],
                lambda b: [V.tensor_tensor(used[:], in_spare[:, QB * E:], used[:], ALU.add)],
                lambda b: [V.tensor_tensor(p1, m1, place, ALU.mult), V.tensor_tensor(p2, m2, place, ALU.mult)],
                lambda b: [V.tensor_reduce(z, ex, AX.X, ALU.add)],
                lambda b: [V.scalar_tensor_tensor(out=z, in0=z, scalar=1e-9, in1=e2, op0=ALU.mult, op1=ALU.add)],
                lambda b: [V.tensor_scalar(z, z, 1.0, None, ALU.add)],
                lambda b: [V.reciprocal(g(b, 0), z)],
                lambda b: [V.tensor_tensor(g(b, 1), e2, g(b, 0), ALU.mult)],
            ]
            assert len(ROUTING) == ROUTE

            def route(b, n):
                if not b.exists(NB):
                    return
                need(dve, sem("route"), ROUTE, b, n)
                if n == 0:
                    need(dve, freed("lg"), 1, b, 1)
                    if not b.loop and b.value == 0:
                        dve.wait_ge(sem("zrow_ready"), 1)
                if n == 1:
                    need(dve, sem("gate_exp"), 2, b, 0)
                if n == 11:
                    need(dve, ready("rk"), 1, b, 0)
                if n == 15:
                    need(dve, sem("gate_exp"), 2, b, 1)
                if n == 16:
                    need(dve, sem("gate_exp"), 2, b, 2)
                if n == 12:
                    need(dve, ready("rk"), 1, b, 1)
                ROUTING[n](b)[-1].then_inc(sem("route"), 1)

            def rows_of(b):
                if not b.exists(NB):
                    return
                need(dve, sem("route"), ROUTE, b, 15)
                with nc.allow_low_precision(reason="row numbers, whole and under 2**24"):
                    V.tensor_reduce(slot[:, b.parity, 0], p1, AX.X, ALU.add)
                    V.tensor_reduce(slot[:, b.parity, 1], p2, AX.X, ALU.add).then_inc(sem("slot_ready"), 1)

            def body(i):
                nxt, prev, rb, late = i.plus(1), i.plus(-1), i.plus(-2), i.plus(-3)
                for h in range(NH):
                    mb, mg = (i, h // 4 + 2) if h < 8 else (i.plus(1), h // 4 - 2)
                    mu = 6 * mg + 3 * (h % 4 // 2)
                    gb, gg = ((i, 1), (i, 2), (i, 3), (nxt, 0))[h // 4]
                    for half in range(2):
                        at = 2 * h + half
                        if at in (2 * LG_STEP + 1, 2 * RK_STEP + 1) and mb.exists(NB):
                            need(dve, sem("max_scores"), AUNITS, mb, mu + 2)
                        if at == 2 * LG_STEP + 1 and rb.exists(NB):
                            need(dve, ready("lg"), 1, rb, 1)
                            V.tensor_copy(lg[:], in_spare[:, 0:QB * E].rearrange(
                                "p (q e) -> p q e", e=E)).then_inc(freed("lg"), 1)
                        if at == 2 * RK_STEP + 1:
                            route(late, 12)
                            route(late, 13)
                        if h % 4 == 0 and not half:
                            split_max(gb, gg, False)
                        if h % 2 == 0:
                            maximum(mb, mu + half, 0)
                        else:
                            maximum(mb, mu + 2, half)
                        if h % 4 == 0 and not half:
                            split_max(gb, gg, True)
                        if h % 4 == 1 and not half:
                            copy_max(gb, gg)
                        if at >= 26:
                            route(rb, at - 26)
                        if at < 6:
                            route(late, 6 + at)
                        if at == 10:
                            route(late, 14)
                        if at == 11:
                            rows_of(late)
                        if 12 <= at < 17:
                            route(late, 3 + at)
                        if nxt.exists(NB):
                            if at == 7:
                                low_part(nxt, qhl, "q", "q_high", "qT")
                            if at == 4:
                                low_part(nxt, khl, "k", "k_high", "kT")
                        if prev.exists(NB):
                            if at == 13:
                                divide(prev, 1, False)
                                divide(prev, 1, True)
                            if at == 24:
                                need(dve, ready("wo"), 1, prev, 1)
                                need(dve, sem("xbo_ready"), 1, prev, 1)
                                V.tensor_tensor(ysum[:], ps_m[:].rearrange("p (q d) -> p q d", q=QB),
                                                xbo[:, prev.parity], ALU.add).then_inc(freed("wo"), 1)
                            if at == 26:
                                need(dve, freed("wo"), 1, prev, 1)
                                statistics(prev, 0, ysum)
                            if at == 27:
                                aggregate(prev, 0)
                        if rb.exists(NB):
                            if at == 4:
                                need(dve, sem("x1_ready"), 1, rb, 1)
                                statistics(rb, 1, x1)
                            if at == 5:
                                aggregate(rb, 1)
                        if i.exists(NB) and at == 29:
                            divide(i, 0, False)
                            divide(i, 0, True)

            iterations(dve, body)

            step = [0]

            def link(ins):
                step[0] += 1
                ins.then_inc(sem("plan_steps"), 1)
                dve.wait_ge(sem("plan_steps"), step[0])

            c, whole, coef, ends, ones8 = (cnt[:, k] for k in range(5))
            dve.wait_ge(sem("route"), ROUTE * NB)
            V.tensor_copy(cnt_i[:, 2], used[0:1, :]).then_inc(sem("ends_ready"), 1)
            V.memset(ones8, 1.0)
            link(V.tensor_tensor(c, used[0:1, :], first_row[0:1, :], ALU.subtract))
            link(V.tensor_scalar(c, c, float(P - 1), None, ALU.add))
            link(V.tensor_copy(cnt_i[:, 0], c))
            link(V.tensor_scalar(cnt_i[:, 1], cnt_i[:, 0], 7, None, ALU.arith_shift_right))
            link(V.tensor_copy(whole, cnt_i[:, 1]))
            V.tensor_scalar(coef, whole, -float(P), float(REG), ALU.mult, ALU.add)
            link(V.tensor_tensor_scan(ends, ones8, whole, 0.0, ALU.mult, ALU.add))
            expert, row, past = (plan[:, k] for k in range(3))
            V.memset(expert, 0.0)
            link(V.tensor_scalar(row, tile_f[0:1, :], float(P), None, ALU.mult))
            for e in range(E):
                V.tensor_scalar(past, tile_f[0:1, :], ends[:, e:e + 1], coef[:, e:e + 1], ALU.is_ge, ALU.mult)
                link(V.scalar_tensor_tensor(out=expert, in0=tile_f[0:1, :], scalar=ends[:, e:e + 1], in1=expert,
                                            op0=ALU.is_ge, op1=ALU.add))
                link(V.tensor_tensor(row, row, past, ALU.add))
            link(V.tensor_scalar(expert, expert, float(E - 1), None, ALU.min))
            V.tensor_copy(plan_i[:, 0], row)
            V.tensor_copy(plan_i[:, 1], expert).then_inc(sem("plan_ready"), 1)

            dve.wait_ge(sem("b1_turned"), 1)
            V.tensor_copy(b1_s[:].rearrange("p e c -> p (e c)"), ps_m[:, 0:E * FC]).then_inc(sem("b1_ready"), 1)
            dve.wait_ge(sem("plan_ready"), 1)
            dve.wait_ge(sem("experts_in"), 16 * (E + 2))

            def weights(j, t):
                e = dve.value_load(plan_i[0:1, 1, bass.ds(j + t, 1)], min_val=0, max_val=E - 1)
                wait_from(dve, sem("h_ready"), j, t - 1)
                V.tensor_copy(w1_t[:, t % 2, :],
                              w1_s[:, bass.ds(e, 1), :].rearrange("p a f -> p (a f)")).then_inc(sem("w1_ready"), 1)

            def turned(j, t):
                dve.wait_ge(sem("tile_turned"), j + (t + 1))
                wait_from(dve, sem("h_ready"), j, t - 3)
                V.tensor_copy(xst[:, t % 4, :], (ps_m, ps_v)[t % 2][:, 0:P]).then_inc(sem("xst_ready"), 1)

            def result(j, t):
                e = dve.value_load(plan_i[0:1, 1, bass.ds(j + t, 1)], min_val=0, max_val=E - 1)
                dve.wait_ge(sem("y_ready"), j + (t + 1))
                before = j * (16 // RING) + 16 * (t // RING)
                if not (isinstance(j, int) and before <= 0):
                    dve.wait_ge(sem(f"sent{t % RING}"), before)
                V.tensor_tensor(ys[:, t % RING, :], ps_s[:, t % 2, 0:D],
                                b2_b[:, bass.ds(e, 1), :].rearrange("p a d -> p (a d)"),
                                ALU.add).then_inc(sem("ys_ready"), 1)

            def tile(j, t):
                at = j + t if isinstance(j, int) else None
                if at is None or at < NT - 1:
                    weights(j, t + 1)
                if at is None or at < NT - 2:
                    turned(j, t + 2)
                if at is None or at >= 1:
                    result(j, t - 1)
                if at == NT - 1:
                    result(j, t)

            weights(0, 0)
            turned(0, 0)
            turned(0, 1)
            tiles(dve, tile)

            def add_choice(b, r, k):
                if k == 0:
                    dve.wait_ge(sem(f"y_in{r}"), b * 8 + 32)
                    if not isinstance(b, int):
                        dve.wait_ge(sem("o_ready"), b + (r - 3))
                else:
                    dve.wait_ge(sem("z_half"), b + (r + 1))
                yt = y_t[:, r].rearrange("p (q k d) -> p q k d", q=QB, k=TOPK)
                xt2 = x2_t[:, r].rearrange("p (q d) -> p q d", q=QB)
                for q in range(QB):
                    gate = gates[:, bass.ds(b * QB + (r * QB + q), 1), k]
                    ins = V.scalar_tensor_tensor(out=z_t[:, r, q, :], in0=yt[:, q, k, :], scalar=gate,
                                                 in1=z_t[:, r, q, :] if k else xt2[:, q, :],
                                                 op0=ALU.mult, op1=ALU.add)
                ins.then_inc(sem("z_done" if k else "z_half"), 1)

            def last_statistics(b, r):
                dve.wait_ge(sem("z_done"), b + (r + 1))
                for q in range(QB):
                    ins = V.bn_stats(zst[:, r % 4, q, :], z_t[:, r % 4, q, :])
                ins.then_inc(sem("zstats"), 1)

            def last_aggregate(b, r):
                wait_apart(dve, sem("dve_passed"), sem("zstats"), b + (r + 1))
                for q in range(QB):
                    ins = V.bn_aggr(zmv[:, r % 4, q, :], zst[:, r % 4, q, :])
                ins.then_inc(sem("zvar"), 1)

            def last_sum(b, r):
                first = isinstance(b, int) and b + r == 0
                add_choice(b, r, 0)
                if not first:
                    last_statistics(b, r - 1)
                add_choice(b, r, 1)
                if not first:
                    last_aggregate(b, r - 1)

            for r in range(4):
                last_sum(0, r)
            with dve.Fori(4, NB - 3, 4) as b:
                for r in range(4):
                    last_sum(b, r)
            last_statistics(NB - 4, 3)
            last_aggregate(NB - 4, 3)


def kernel(**inputs):
    import numpy as np
    import concourse.bacc as bacc
    from concourse.bass_utils import run_bass_kernel_spmd

    names = ["L0_attn_x", "L0_attn_Wq", "L0_attn_Wk", "L0_attn_Wv", "L0_attn_Wo", "L0_attn_bo", "L0_ffn_gamma",
             "L0_ffn_beta", "L0_ffn_Wg", "L0_ffn_W1", "L0_ffn_b1", "L0_ffn_W2", "L0_ffn_b2"]
    nc = bacc.Bacc("TRN2", target_bir_lowering=False, num_devices=1)
    arrays = {n: np.ascontiguousarray(inputs[n]) for n in names}
    args = [nc.dram_tensor(n, arrays[n].shape, mybir.dt.from_np(arrays[n].dtype), kind="ExternalInput").ap()
            for n in names]
    out = nc.dram_tensor("out", arrays[names[0]].shape, F32, kind="ExternalOutput").ap()
    build_program(nc, *args, out)
    return run_bass_kernel_spmd(nc, [arrays], core_ids=[0]).results[0]["out"]
```
